# Optimizing a Trainium2 kernel written in Bass

```python
import numpy as np
import jax
import jax.numpy as jnp

def _softmax(x, axis=-1):
    return jax.nn.softmax(x, axis=axis)

def _gelu(x):
    return jax.nn.gelu(x, approximate=True)

def _silu(x):
    return jax.nn.silu(x)

def _sigmoid(x):
    return jax.nn.sigmoid(x)

def _layernorm(x, axis=-1, eps=1e-05):
    m = jnp.mean(x, axis=axis, keepdims=True)
    v = jnp.var(x, axis=axis, keepdims=True)
    return (x - m) / jnp.sqrt(v + eps)

def _scatter_add(tgt, idx, src, axis=0):
    return tgt.at[idx].add(src)

def _segment_sum(src, seg, n):
    return jax.ops.segment_sum(src, seg, n)
kernel_name = 'mk_adj_resnorm_d1_adj_r2_8ebe4a'

def setup_inputs(seed: int=0):
    np.random.seed(seed)
    _w = jnp.asarray

    def _rec_inputs():
        import jax
        import jax.numpy as jnp
        _gk = jax.random.key(seed)
        x = -0.003407 + 1.001 * jax.random.normal(jax.random.fold_in(_gk, 1), (32, 256, 128), jnp.float32)
        _a = jax.random.bernoulli(jax.random.fold_in(_gk, 2), 0.0078125, (32, 256, 256))
        _a = jnp.logical_or(_a, jnp.swapaxes(_a, -1, -2))
        _a = jnp.logical_or(_a, jnp.eye(256, dtype=bool))
        _af = _a.astype(jnp.float32)
        _af = _af * jax.random.uniform(jax.random.fold_in(_gk, 3), (32, 256, 256), jnp.float32, 0.05, 0.999994)
        adj = _af
        return (x, adj)
    x, adj = _rec_inputs()

    def _L0_gnn_setup():
        import jax, jax.numpy as jnp
        import numpy as np
        LN_EPS = 1e-05

        def _layernorm(x, gamma, beta):
            mu = jnp.mean(x, axis=-1, keepdims=True)
            var = jnp.mean(jnp.square(x - mu), axis=-1, keepdims=True)
            return (x - mu) * jax.lax.rsqrt(var + LN_EPS) * gamma + beta
        key = jax.random.key(seed)
        ks = jax.random.split(key, 10)
        B, N, D, O = (2, 256, 128, 128)
        node_features = jax.random.normal(ks[0], (B, N, D), dtype=jnp.float32)
        adjacency = jax.random.uniform(ks[1], (B, N, N), dtype=jnp.float32)
        s1 = 1.0 / np.sqrt(2 * D)
        s2 = 1.0 / np.sqrt(D + O)
        W1 = jax.random.uniform(ks[2], (2 * D, O), jnp.float32, -s1, s1)
        b1 = jax.random.uniform(ks[3], (O,), jnp.float32, -s1, s1)
        g1 = jnp.ones((O,), jnp.float32)
        be1 = jnp.zeros((O,), jnp.float32)
        W2 = jax.random.uniform(ks[4], (D + O, O), jnp.float32, -s2, s2)
        b2 = jax.random.uniform(ks[5], (O,), jnp.float32, -s2, s2)
        g2 = jnp.ones((O,), jnp.float32)
        be2 = jnp.zeros((O,), jnp.float32)
        return {'node_features': node_features, 'adjacency': adjacency, 'W1': W1, 'b1': b1, 'g1': g1, 'be1': be1, 'W2': W2, 'b2': b2, 'g2': g2, 'be2': be2}
    _L0_gnn_all = _L0_gnn_setup()
    _L0_gnn_in = {k: v for k, v in _L0_gnn_all.items() if k in ('W1', 'b1', 'g1', 'be1', 'W2', 'b2', 'g2', 'be2')}
    del _L0_gnn_all
    return {'x': x, 'adj': adj, 'L0_gnn_W1': _L0_gnn_in['W1'], 'L0_gnn_b1': _L0_gnn_in['b1'], 'L0_gnn_g1': _L0_gnn_in['g1'], 'L0_gnn_be1': _L0_gnn_in['be1'], 'L0_gnn_W2': _L0_gnn_in['W2'], 'L0_gnn_b2': _L0_gnn_in['b2'], 'L0_gnn_g2': _L0_gnn_in['g2'], 'L0_gnn_be2': _L0_gnn_in['be2']}

def reference(x, adj, L0_gnn_W1, L0_gnn_b1, L0_gnn_g1, L0_gnn_be1, L0_gnn_W2, L0_gnn_b2, L0_gnn_g2, L0_gnn_be2):
    import jax
    import jax.numpy as jnp

    def _L0_gnn_ref(node_features, adjacency, W1, b1, g1, be1, W2, b2, g2, be2):
        import jax, jax.numpy as jnp
        import numpy as np
        LN_EPS = 1e-05

        def _layernorm(x, gamma, beta):
            mu = jnp.mean(x, axis=-1, keepdims=True)
            var = jnp.mean(jnp.square(x - mu), axis=-1, keepdims=True)
            return (x - mu) * jax.lax.rsqrt(var + LN_EPS) * gamma + beta
        B, N, D = node_features.shape
        m_j = jnp.einsum('bnd,do->bno', node_features, W1[:D])
        m_i = jnp.einsum('bnd,do->bno', node_features, W1[D:])
        pre = m_j[:, None, :, :] + m_i[:, :, None, :] + b1
        msg = jax.nn.gelu(_layernorm(pre, g1, be1), approximate=False)
        agg = jnp.einsum('bijo,bij->bio', msg, adjacency)
        upd_in = jnp.concatenate([node_features, agg], axis=-1)
        updated = _layernorm(upd_in @ W2 + b2, g2, be2)
        return updated
    x = _layernorm(x + _L0_gnn_ref(x, adj, L0_gnn_W1, L0_gnn_b1, L0_gnn_g1, L0_gnn_be1, L0_gnn_W2, L0_gnn_b2, L0_gnn_g2, L0_gnn_be2), axis=-1)
    return x

_drawn_inputs = setup_inputs


def setup_inputs(seed=0):
    import zlib

    import numpy as np

    out = dict(_drawn_inputs(seed))
    spreads = {'L0_gnn_g1': (1.0, 0.2),
     'L0_gnn_be1': (0.0, 0.1),
     'L0_gnn_g2': (1.0, 0.2),
     'L0_gnn_be2': (0.0, 0.1)}
    factors = {}
    for name, (base, spread) in spreads.items():
        noise = np.random.default_rng([zlib.crc32(name.encode()), seed]).standard_normal(out[name].shape)
        drawn = base * np.exp(spread * noise) if base else spread * noise
        out[name] = jnp.asarray(drawn.astype(out[name].dtype))
    for name, factor in factors.items():
        out[name] = (out[name] * factor).astype(out[name].dtype)
    return out
```

```python
import math
from collections import namedtuple
from contextlib import ExitStack

import concourse.bass as bass
from concourse import mybir

B, N, D, O = 32, 256, 128, 128
P = 128
NH = N // P
LN_EPS = 1e-5

FAST_STEPS = [(h, slots) for h in range(NH) for slots in ((0, 1, 2, 3), (4, 5, 6, 7), (8, 9, 10, 11), (12, 13, 14))]
FAST_CAP = [15, 15]
NBANK = 4
GEN_SLOTS = 12
GEN_STEPS = [(0, 1, 2), (3, 4, 5), (6, 7, 8), (9, 10, 11)]
GEN_ROUNDS = -(-N // GEN_SLOTS)
EXTRACTED = 16

Graph = namedtuple("Graph", "b n par m back")
Step = namedtuple("Step", "s a bank h slots")


def gnn_kernel(nc, x, xt, adj, W1, b1, g1, be1, W2, b2, g2, be2, out):
    fp32, bf16, i32, u16 = mybir.dt.float32, mybir.dt.bfloat16, mybir.dt.int32, mybir.dt.uint16
    ALU, ACT, AX = mybir.AluOpType, mybir.ActivationFunctionType, mybir.AxisListType
    S = len(FAST_STEPS)
    KTOT = sum(len(slots) for _, slots in FAST_STEPS)

    ctx = ExitStack()
    with ctx:
        def sb(name, shape, dt=fp32):
            return ctx.enter_context(nc.sbuf_tensor(name, shape, dt))

        def ps(name, shape, dt=fp32):
            return ctx.enter_context(nc.psum_tensor(name, shape, dt))

        def sem(name):
            return ctx.enter_context(nc.semaphore(name))

        ident = sb("ident", [P, P], bf16)
        ident32 = sb("ident32", [P, P])
        upto = sb("upto", [P, P], bf16)
        ones = sb("ones", [P, P], bf16)
        ones_row = sb("ones_row", [1, P])
        order = sb("order", [P, NH, N])
        order_i = sb("order_i", [P, NH, N], i32)
        minus_half = sb("minus_half", [P, 4])
        eps = sb("eps", [P, 4])
        eps_o = sb("eps_o", [P, 4])
        slot_no = sb("slot_no", [P, GEN_SLOTS])
        slot_i = sb("slot_i", [P, GEN_SLOTS], i32)
        w1 = sb("w1", [P, 2, O])
        w1sum = sb("w1sum", [P, 2])
        w1c = sb("w1c", [P, 2, O])
        w2 = sb("w2", [P, 2, O])
        b1r = sb("b1r", [1, O])
        b1sum = sb("b1sum", [1, 1])
        b1c = sb("b1c", [1, O])
        b2r = sb("b2r", [1, O])
        g1b = sb("g1b", [P, O])
        g1o = sb("g1o", [P, O])
        be1b = sb("be1b", [P, O])
        g2b = sb("g2b", [P, O])
        be2b = sb("be2b", [P, O])

        adj_sb = sb("adj_sb", [P, 2, NH, N])
        xt_sb = sb("xt_sb", [P, 2, N])
        x_sb = sb("x_sb", [P, 2, NH, D])
        mask = sb("mask", [P, NH, N], bf16)
        mask_t = sb("mask_t", [P, NH, N], bf16)
        rank_t = sb("rank_t", [P, 2, NH, N], bf16)
        tab = sb("tab", [P, 2, 3, NH, 2 * O], bf16)
        rest = sb("rest", [P, NH, 2 * O])
        adj_n = sb("adj_n", [P, NH, N])
        halves = sb("halves", [P, 2, NH, N])
        place = sb("place", [P, NH, N])
        key = sb("key", [P, 2, NH, N])
        key2 = sb("key2", [P, NH, 2, N])
        top = sb("top", [P, 2, NH, 2, EXTRACTED])
        top_i = sb("top_i", [P, NH, 2, EXTRACTED], i32)
        wgt = sb("wgt", [P, 2, NH, EXTRACTED])
        agg = sb("agg", [P, 2, NH, O])
        agg_t = sb("agg_t", [P, NH, P])
        over = sb("over", [P, NH, 2])

        onehot = sb("onehot", [P, NBANK, 4, NH, P], bf16)
        squares = sb("squares", [P, NBANK, 4, O], bf16)
        ssq = sb("ssq", [P, NBANK, 4])
        var1 = sb("var1", [P, NBANK, 4])
        rstd = sb("rstd", [P, NBANK, 4])
        msg = sb("msg", [P, NBANK, 4, O])

        stats = sb("stats", [P, NH, 6])
        moments = sb("moments", [P, NH, 2])
        veps = sb("veps", [P, NH])
        rstd2 = sb("rstd2", [P, NH])
        upd = sb("upd", [P, NH, O])
        stats3 = sb("stats3", [P, NH, 6])
        moments3 = sb("moments3", [P, NH, 2])
        veps3 = sb("veps3", [P, NH])
        rstd3 = sb("rstd3", [P, NH])
        y = sb("y", [P, 2, NH, O])
        carrier = sb("carrier", [P, 5])
        over1 = sb("over1", [P, 1])
        over2 = sb("over2", [1, 1])
        flag = sb("flag", [1, 1], i32)

        pre = [ps(f"pre{i}", [P, 4, O]) for i in range(NBANK)]
        mask_ps = ps("mask_ps", [P, NH, N], bf16)
        rank_ps = ps("rank_ps", [P, NH, N])
        tab_ps = ps("tab_ps", [P, NH, 2 * O])
        end_ps = ps("end_ps", [P, 2, NH, P])

        weights_in = sem("weights_in")
        consts_pool = sem("consts_pool")
        consts_dve = sem("consts_dve")
        adj_in = [sem("adj_in0"), sem("adj_in1")]
        xt_in = [sem("xt_in0"), sem("xt_in1")]
        x_in = [sem("x_in0"), sem("x_in1")]
        mask_done = sem("mask_done")
        maskt_ps = sem("maskt_ps")
        maskt_sb = sem("maskt_sb")
        rank_psd = sem("rank_psd")
        rank_done = sem("rank_done")
        tab_psd = sem("tab_psd")
        hi_done = sem("hi_done")
        rest_done = sem("rest_done")
        mid_done = sem("mid_done")
        tab_done = sem("tab_done")
        adjn_done = sem("adjn_done")
        place_done = sem("place_done")
        halves_done = sem("halves_done")
        keys_done = sem("keys_done")
        top8 = sem("top8")
        cut = sem("cut")
        top_done = sem("top_done")
        topi_done = sem("topi_done")
        wgt_done = sem("wgt_done")
        over_done = sem("over_done")
        onehot_done = sem("onehot_done")
        pre_done = sem("pre_done")
        ssq_done = sem("ssq_done")
        var_done = sem("var_done")
        rstd_done = sem("rstd_done")
        norm_done = sem("norm_done")
        shift_done = sem("shift_done")
        gelu_done = sem("gelu_done")
        acc_done = sem("acc_done")
        aggt_ps = sem("aggt_ps")
        aggt_sb = sem("aggt_sb")
        upd_ps = sem("upd_ps")
        st_done = sem("st_done")
        mom_done = sem("mom_done")
        veps_done = sem("veps_done")
        rstd2_done = sem("rstd2_done")
        updn_done = sem("updn_done")
        y_steps = sem("y_steps")
        st3_done = sem("st3_done")
        mom3_done = sem("mom3_done")
        veps3_done = sem("veps3_done")
        rstd3_done = sem("rstd3_done")
        y_done = sem("y_done")
        out_written = [sem("out_written0"), sem("out_written1")]
        over_red = sem("over_red")
        over_t = sem("over_t")
        over_max = sem("over_max")
        flag_done = sem("flag_done")
        gen_kept = sem("gen_kept")
        gen_slot = sem("gen_slot")

        def wait(eng, s, value):
            if not isinstance(value, int) or value > 0:
                eng.wait_ge(s, value)


        def load_adj(G):
            wait(nc.sync, mask_done, G.n - G.back)
            wait(nc.sync, adjn_done, G.n - G.back)
            nc.sync.dma_start(adj_sb[:, G.par], adj[G.b].rearrange("(h p) j -> p h j", p=P)).then_inc(adj_in[G.par], 16)

        def load_xt(G):
            wait(nc.sync, tab_psd, G.n - G.back)
            wait(nc.sync, upd_ps, G.n - G.back)
            nc.sync.dma_start(xt_sb[:, G.par], xt[G.b]).then_inc(xt_in[G.par], 16)

        def load_x(G):
            wait(nc.sync, y_steps, 3 * (G.n - G.back))
            nc.sync.dma_start(x_sb[:, G.par], x[G.b].rearrange("(h p) d -> p h d", p=P)).then_inc(x_in[G.par], 16)

        def store_y(G):
            nc.sync.wait_ge(y_done, G.n)
            nc.sync.dma_start(out[G.b].rearrange("(h p) o -> p h o", p=P), y[:, G.par]).then_inc(out_written[G.par], 16)

        def transpose_mask(G):
            nc.tensor.wait_ge(mask_done, G.n)
            wait(nc.tensor, maskt_sb, G.n - 1)
            for h in range(NH):
                for jb in range(NH):
                    last = nc.tensor.transpose(mask_ps[:, jb, h * P:(h + 1) * P], mask[:, h, jb * P:(jb + 1) * P], ident[:, :])
            last.then_inc(maskt_ps, 1)

        def rank_product(G):
            nc.tensor.wait_ge(maskt_sb, G.n)
            wait(nc.tensor, rank_done, G.n - 1)
            nc.tensor.matmul(rank_ps[:, 0, :], upto[:, :], mask_t[:, 0, :], start=True, stop=True)
            nc.tensor.matmul(rank_ps[:, 1, :], ones[:, :], mask_t[:, 0, :], start=True, stop=False)
            nc.tensor.matmul(rank_ps[:, 1, :], upto[:, :], mask_t[:, 1, :], start=False, stop=True).then_inc(rank_psd, 1)

        def table_product(G):
            nc.tensor.wait_ge(xt_in[G.par], 16 * G.m)
            wait(nc.tensor, rest_done, G.n - 1)
            for h in range(NH):
                nc.tensor.matmul(tab_ps[:, h, :], xt_sb[:, G.par, h * P:(h + 1) * P],
                                 w1c[:, :, :].rearrange("p a o -> p (a o)"), start=True, stop=False, skip_group_check=True)
                last = nc.tensor.matmul(tab_ps[:, h, O:2 * O], ones_row[:, :], b1c[:, :], start=False, stop=True, skip_group_check=True)
            last.then_inc(tab_psd, 1)

        def gather(G, T):
            nc.tensor.wait_ge(onehot_done, T.s + 1)
            nc.tensor.wait_ge(tab_done, G.n)
            wait(nc.tensor, norm_done, T.s - NBANK + 1)
            kn = len(T.slots)
            for part in range(3):
                nc.tensor.matmul(pre[T.bank][:, 0:kn, :], ident[:, :],
                                 tab[:, G.par, part, T.h, O:2 * O].unsqueeze(1).to_broadcast([P, kn, O]),
                                 start=(part == 0), stop=False, skip_group_check=True)
            for q in range(kn):
                for jb in range(NH):
                    for part in range(3):
                        last = nc.tensor.matmul(pre[T.bank][:, q, :], onehot[:, T.bank, q, jb, :],
                                                tab[:, G.par, part, jb, 0:O], start=False,
                                                stop=(jb == NH - 1 and part == 2), skip_group_check=True)
            last.then_inc(pre_done, 1)

        def transpose_agg(G, a_end):
            nc.tensor.wait_ge(acc_done, a_end)
            wait(nc.tensor, updn_done, G.n - 1)
            for h in range(NH):
                last = nc.tensor.transpose(end_ps[:, 0, h, :], agg[:, G.par, h, :], ident32[:, :])
            last.then_inc(aggt_ps, 1)

        def update_product(G):
            nc.tensor.wait_ge(aggt_sb, G.n)
            for h in range(NH):
                nc.tensor.matmul(end_ps[:, 1, h, :], xt_sb[:, G.par, h * P:(h + 1) * P], w2[:, 0, :], start=True, stop=False)
                nc.tensor.matmul(end_ps[:, 1, h, :], agg_t[:, h, :], w2[:, 1, :], start=False, stop=False)
                last = nc.tensor.matmul(end_ps[:, 1, h, :], ones_row[:, :], b2r[:, :], start=False, stop=True)
            last.then_inc(upd_ps, 1)

        def copy_mask(G):
            nc.scalar.wait_ge(maskt_ps, G.n)
            wait(nc.scalar, rank_done, G.n - 1)
            nc.scalar.copy(mask_t[:, :, :], mask_ps[:, :, :]).then_inc(maskt_sb, 1)

        def split_bits(G):
            nc.scalar.wait_ge(adj_in[G.par], 16 * G.m)
            nc.scalar.activation(adj_n[:, :, :], adj_sb[:, G.par], ACT.Identity).then_inc(adjn_done, 1)
            nc.scalar.wait_ge(adjn_done, G.n)
            wait(nc.scalar, keys_done, G.n - 1)
            bits = adj_n[:, :, :].bitcast(u16).rearrange("p h (j t) -> p t h j", t=2)
            nc.scalar.copy(halves[:, 0], bits[:, 0])
            nc.scalar.copy(halves[:, 1], bits[:, 1]).then_inc(halves_done, 1)

        def table_hi(G, s_free):
            nc.scalar.wait_ge(tab_psd, G.n)
            wait(nc.scalar, pre_done, s_free)
            nc.scalar.copy(tab[:, G.par, 0], tab_ps[:, :, :]).then_inc(hi_done, 1)

        def table_mid(G):
            nc.scalar.wait_ge(rest_done, G.n)
            nc.scalar.copy(tab[:, G.par, 1], rest[:, :, :]).then_inc(mid_done, 1)

        def square(T):
            nc.scalar.wait_ge(pre_done, T.s + 1)
            wait(nc.scalar, var_done, T.s - NBANK + 1)
            for q in range(len(T.slots)):
                last = nc.scalar.activation(squares[:, T.bank, q, :], pre[T.bank][:, q, :], ACT.Square, accum_out=ssq[:, T.bank, q:q + 1])
            last.then_inc(ssq_done, 1)

        def gelu(T):
            nc.scalar.wait_ge(shift_done, T.s + 1)
            kn = len(T.slots)
            nc.scalar.activation(msg[:, T.bank, 0:kn, :], msg[:, T.bank, 0:kn, :], ACT.Gelu).then_inc(gelu_done, 1)

        def make_weights(G, t, wgt_free):
            act = nc.scalar
            act.wait_ge(top_done, t)
            wait(act, wgt_done, t - 1)
            wait(act, acc_done, wgt_free)
            act.copy(top_i[:, :, :, :], top[:, G.par]).then_inc(topi_done, 1)
            act.wait_ge(topi_done, t)
            low = top_i[:, :, :, :].bitcast(u16).rearrange("p h t (k u) -> p u t h k", u=2)
            to = wgt[:, G.par].bitcast(u16).rearrange("p h (k u) -> p u h k", u=2)
            act.copy(to[:, 1], low[:, 0, 0])
            act.copy(to[:, 0], low[:, 0, 1]).then_inc(wgt_done, 1)

        def copy_agg_t(G):
            nc.scalar.wait_ge(aggt_ps, G.n)
            wait(nc.scalar, upd_ps, G.n - 1)
            nc.scalar.copy(agg_t[:, :, :], end_ps[:, 0]).then_inc(aggt_sb, 1)

        def make_keys(G, top_free):
            pool = nc.gpsimd
            pool.wait_ge(mask_done, G.n)
            pool.tensor_tensor(place[:, :, :], mask[:, :, :], order[:, :, :], ALU.mult).then_inc(place_done, 1)
            pool.wait_ge(place_done, G.n)
            wait(pool, top_done, top_free)
            pool.wait_ge(halves_done, G.n)
            pool.tensor_tensor(key[:, 0], place[:, :, :], halves[:, 1], ALU.add)
            pool.tensor_tensor(key[:, 1], place[:, :, :], halves[:, 0], ALU.add).then_inc(keys_done, 1)

        def table_rest(G):
            pool = nc.gpsimd
            pool.wait_ge(mid_done, G.n)
            pool.tensor_tensor(tab[:, G.par, 2], rest[:, :, :], tab[:, G.par, 1], ALU.subtract).then_inc(tab_done, 1)

        def rsqrt(T):
            pool = nc.gpsimd
            kn = len(T.slots)
            pool.wait_ge(ssq_done, T.s + 1)
            pool.tensor_tensor(var1[:, T.bank, 0:kn], ssq[:, T.bank, 0:kn], eps_o[:, 0:kn], ALU.add).then_inc(var_done, 1)
            pool.wait_ge(var_done, T.s + 1)
            wait(pool, norm_done, T.s - NBANK + 1)
            pool.tensor_tensor(rstd[:, T.bank, 0:kn], var1[:, T.bank, 0:kn], minus_half[:, 0:kn], ALU.pow).then_inc(rstd_done, 1)

        def shift(T):
            pool = nc.gpsimd
            kn = len(T.slots)
            pool.wait_ge(norm_done, T.s + 1)
            m = msg[:, T.bank, 0:kn, :]
            pool.tensor_tensor(m, m, be1b[:, :].unsqueeze(1).to_broadcast([P, kn, O]), ALU.add).then_inc(shift_done, 1)

        def rstd_update(G):
            pool = nc.gpsimd
            pool.wait_ge(mom_done, G.n)
            pool.tensor_tensor(veps[:, :], moments[:, :, 1], eps[:, 0:NH], ALU.add).then_inc(veps_done, 1)
            pool.wait_ge(veps_done, G.n)
            pool.tensor_tensor(rstd2[:, :], veps[:, :], minus_half[:, 0:NH], ALU.pow).then_inc(rstd2_done, 1)

        def residual(G):
            pool = nc.gpsimd
            def wide(v):
                return v[:, :].unsqueeze(1).to_broadcast([P, NH, O])
            pool.wait_ge(updn_done, G.n)
            wait(pool, out_written[G.par], 16 * (G.m - 1))
            pool.tensor_tensor(y[:, G.par], upd[:, :, :], wide(g2b), ALU.mult).then_inc(y_steps, 1)
            pool.wait_ge(y_steps, 3 * G.n - 2)
            pool.tensor_tensor(y[:, G.par], y[:, G.par], wide(be2b), ALU.add).then_inc(y_steps, 1)
            pool.wait_ge(y_steps, 3 * G.n - 1)
            pool.wait_ge(x_in[G.par], 16 * G.m)
            pool.tensor_tensor(y[:, G.par], y[:, G.par], x_sb[:, G.par], ALU.add).then_inc(y_steps, 1)

        def rstd_out(G):
            pool = nc.gpsimd
            pool.wait_ge(mom3_done, G.n)
            pool.tensor_tensor(veps3[:, :], moments3[:, :, 1], eps[:, 0:NH], ALU.add).then_inc(veps3_done, 1)
            pool.wait_ge(veps3_done, G.n)
            pool.tensor_tensor(rstd3[:, :], veps3[:, :], minus_half[:, 0:NH], ALU.pow).then_inc(rstd3_done, 1)

        def make_mask(G):
            dve = nc.vector
            dve.wait_ge(adj_in[G.par], 16 * G.m)
            wait(dve, maskt_ps, G.n - 1)
            wait(dve, place_done, G.n - 1)
            dve.tensor_scalar(mask[:, :, :], adj_sb[:, G.par], 0.0, None, ALU.not_equal).then_inc(mask_done, 1)

        def make_rank(G):
            dve = nc.vector
            dve.wait_ge(rank_psd, G.n)
            dve.tensor_tensor(rank_t[:, G.par], rank_ps[:, :, :], mask_t[:, :, :], ALU.mult).then_inc(rank_done, 1)

        def make_rest(G):
            dve = nc.vector
            dve.wait_ge(hi_done, G.n)
            wait(dve, tab_done, G.n - 1)
            dve.tensor_tensor(rest[:, :, :], tab_ps[:, :, :], tab[:, G.par, 0], ALU.subtract).then_inc(rest_done, 1)

        def extract(G, caps, t, keep=None):
            dve = nc.vector
            dve.wait_ge(keys_done, G.n)
            wait(dve, topi_done, t - 1)
            two = [h for h in range(NH) if caps[h] >= 8]
            dve.memset(carrier[:, 0:1], 0.0)
            for h in range(NH):
                for u in range(2):
                    last = dve.max(top[:, G.par, h, u, 0:8], key[:, u, h, :])
            last.then_inc(top8, 1)
            dve.wait_ge(top8, t)
            for i, h in enumerate(two):
                wait(dve, top_done, t - 1)
                for u in range(2):
                    last = dve.scalar_tensor_tensor(key2[:, h, u, :], key[:, u, h, :], top[:, G.par, h, u, 7:8], key[:, u, h, :],
                                                    ALU.is_lt, ALU.mult)
                last.then_inc(cut, 1)
                dve.wait_ge(cut, len(two) * (t - 1) + i + 1)
                dve.memset(carrier[:, 1 + h:2 + h], 0.0)
                for u in range(2):
                    last = dve.max(top[:, G.par, h, u, 8:16], key2[:, h, u, :])
            last.then_inc(top_done, 1)

        def note_over(G, caps):
            dve = nc.vector
            dve.wait_ge(top_done, G.n)
            for h in range(NH):
                wait(dve, over_done, NH * (G.n - 1) + h)
                dve.tensor_tensor(over[:, h, :], over[:, h, :], top[:, G.par, h, :, caps[h]], ALU.max).then_inc(over_done, 1)

        def make_onehot(G, T, slot_ap=False):
            dve = nc.vector
            dve.wait_ge(rank_done, G.n)
            wait(dve, pre_done, T.s - NBANK + 1)
            for q, k in enumerate(T.slots):
                value = slot_no[:, k:k + 1] if slot_ap else float(k + 1)
                last = dve.tensor_scalar(onehot[:, T.bank, q], rank_t[:, G.par, :, T.h * P:(T.h + 1) * P], value, None, ALU.is_equal)
            last.then_inc(onehot_done, 1)

        def norm_slot(T, q):
            dve = nc.vector
            if q == 0:
                dve.wait_ge(rstd_done, T.s + 1)
                wait(dve, gelu_done, T.s - NBANK + 1)
            ins = dve.scalar_tensor_tensor(msg[:, T.bank, q, :], pre[T.bank][:, q, :], rstd[:, T.bank, q:q + 1], g1o[:, :], ALU.mult, ALU.mult)
            if q == len(T.slots) - 1:
                ins.then_inc(norm_done, 1)

        def acc_slot(G, T, q, t, agg_free=None):
            dve = nc.vector
            if q == 0:
                dve.wait_ge(gelu_done, T.s + 1)
                dve.wait_ge(wgt_done, t)
            first = agg_free is not None and T.slots[q] == 0
            if first:
                wait(dve, aggt_ps, agg_free)
            else:
                dve.wait_ge(acc_done, T.a + q)
            a = agg[:, G.par, T.h, :]
            w = wgt[:, G.par, T.h, T.slots[q]:T.slots[q] + 1]
            if first:
                ins = dve.tensor_scalar(a, msg[:, T.bank, q, :], w, None, ALU.mult)
            else:
                ins = dve.scalar_tensor_tensor(a, msg[:, T.bank, q, :], w, a, ALU.mult, ALU.add)
            ins.then_inc(acc_done, 1)

        def update_moments(G):
            dve = nc.vector
            dve.wait_ge(upd_ps, G.n)
            for h in range(NH):
                last = dve.bn_stats(stats[:, h, :], end_ps[:, 1, h, :])
            last.then_inc(st_done, 1)
            dve.wait_ge(st_done, G.n)
            wait(dve, veps_done, G.n - 1)
            dve.memset(carrier[:, 3:4], 0.0)
            for h in range(NH):
                last = dve.bn_aggr(moments[:, h, :], stats[:, h, :])
            last.then_inc(mom_done, 1)

        def update_norm(G):
            dve = nc.vector
            dve.wait_ge(rstd2_done, G.n)
            wait(dve, y_steps, 3 * (G.n - 1))
            for h in range(NH):
                last = dve.tensor_scalar(upd[:, h, :], end_ps[:, 1, h, :], moments[:, h, 0:1], rstd2[:, h:h + 1], ALU.subtract, ALU.mult)
            last.then_inc(updn_done, 1)

        def out_moments(G):
            dve = nc.vector
            dve.wait_ge(y_steps, 3 * G.n)
            for h in range(NH):
                last = dve.bn_stats(stats3[:, h, :], y[:, G.par, h, :])
            last.then_inc(st3_done, 1)
            dve.wait_ge(st3_done, G.n)
            wait(dve, veps3_done, G.n - 1)
            dve.memset(carrier[:, 4:5], 0.0)
            for h in range(NH):
                last = dve.bn_aggr(moments3[:, h, :], stats3[:, h, :])
            last.then_inc(mom3_done, 1)

        def out_norm(G):
            dve = nc.vector
            dve.wait_ge(rstd3_done, G.n)
            for h in range(NH):
                last = dve.tensor_scalar(y[:, G.par, h, :], y[:, G.par, h, :], moments3[:, h, 0:1], rstd3[:, h:h + 1], ALU.subtract, ALU.mult)
            last.then_inc(y_done, 1)


        def graph(g, c):
            return Graph(2 * g + c, 2 * g + c + 1, c % 2, g + c // 2 + 1, 2)

        def step(g, c, i):
            c, i = c + i // S, i % S
            h, slots = FAST_STEPS[i]
            before = sum(len(v) for _, v in FAST_STEPS[:i])
            return graph(g, c), Step((2 * g + c) * S + i, (2 * g + c) * KTOT + before, i % NBANK, h, slots)

        def there(g, c, i=0):
            return not isinstance(g, int) or 0 <= 2 * g + c + i // S < B

        def sp_graph(g, c):
            if there(g, c + 2):
                load_adj(graph(g, c + 2))
            if there(g, c):
                load_x(graph(g, c))
            if there(g, c + 1):
                load_xt(graph(g, c + 1))
            if there(g, c - 2):
                store_y(graph(g, c - 2))

        def pe_graph(g, c):
            for i in range(S):
                if there(g, c):
                    gather(*step(g, c, i))
                if i == 0 and there(g, c + 1):
                    transpose_mask(graph(g, c + 1))
                if i == 1 and there(g, c + 1):
                    rank_product(graph(g, c + 1))
                if i == 3 and there(g, c - 1):
                    transpose_agg(graph(g, c - 1), (2 * g + c) * KTOT)
                if i == 4 and there(g, c - 1):
                    update_product(graph(g, c - 1))
                if i == S - 2 and there(g, c + 1):
                    table_product(graph(g, c + 1))

        def act_graph(g, c):
            for i in range(S):
                if there(g, c, i):
                    square(step(g, c, i)[1])
                if there(g, c, i - 2):
                    gelu(step(g, c, i - 2)[1])
                if i == 1 and there(g, c + 1):
                    copy_mask(graph(g, c + 1))
                if i == 2 and there(g, c + 1):
                    split_bits(graph(g, c + 1))
                if i == 4 and there(g, c - 1):
                    copy_agg_t(graph(g, c - 1))
                if i == S - 2 and there(g, c + 1):
                    make_weights(graph(g, c + 1), 2 * g + c + 2, KTOT * (2 * g + c))
            if there(g, c + 1):
                table_hi(graph(g, c + 1), S * (2 * g + c))
                table_mid(graph(g, c + 1))

        def pool_graph(g, c):
            for i in range(S):
                if there(g, c, i):
                    rsqrt(step(g, c, i)[1])
                if there(g, c, i - 1):
                    shift(step(g, c, i - 1)[1])
                if i == 0 and there(g, c - 2):
                    residual(graph(g, c - 2))
                if i == 1 and there(g, c + 1):
                    make_keys(graph(g, c + 1), 2 * g + c + 1)
                if i == 2 and there(g, c - 2):
                    rstd_out(graph(g, c - 2))
                if i == S - 1 and there(g, c - 1):
                    rstd_update(graph(g, c - 1))
            if there(g, c + 1):
                table_rest(graph(g, c + 1))

        def dve_graph(g, c):
            for i in range(S):
                if there(g, c, i + 1):
                    make_onehot(*step(g, c, i + 1))
                pair = ([lambda q=q: norm_slot(step(g, c, i - 1)[1], q) for q in range(len(step(g, c, i - 1)[1].slots))] if there(g, c, i - 1) else [],
                        [lambda q=q: acc_slot(*step(g, c, i - 3), q, graph(g, c + (i - 3) // S).n, graph(g, c + (i - 3) // S).n - 2)
                         for q in range(len(step(g, c, i - 3)[1].slots))] if there(g, c, i - 3) else [])
                for q in range(4):
                    for ops in pair:
                        if q < len(ops):
                            ops[q]()
                if i == 0 and there(g, c + 1):
                    make_mask(graph(g, c + 1))
                if i == 0 and there(g, c - 2):
                    update_norm(graph(g, c - 2))
                if i == 2 and there(g, c - 2):
                    out_moments(graph(g, c - 2))
                if i == 3 and there(g, c + 1):
                    make_rank(graph(g, c + 1))
                if i == 4 and there(g, c - 2):
                    out_norm(graph(g, c - 2))
                if i == 4 and there(g, c + 1):
                    extract(graph(g, c + 1), FAST_CAP, 2 * g + c + 2)
                if i == 5 and there(g, c + 1):
                    note_over(graph(g, c + 1), FAST_CAP)
                if i == S - 2 and there(g, c - 1):
                    update_moments(graph(g, c - 1))
            if there(g, c + 1):
                make_rest(graph(g, c + 1))

        def fast_pass(eng, one_graph):
            for c in (-2, -1, 0, 1):
                one_graph(0, c)
            with eng.Fori(1, B // 2 - 1) as g:
                one_graph(g, 0)
                one_graph(g, 1)
            for c in range(4):
                one_graph(B // 2 - 1, c)


        GR = GEN_ROUNDS
        A0 = B * KTOT
        S0 = B * S
        SG = NH * GR * len(GEN_STEPS)
        AG = NH * GR * GEN_SLOTS
        GSTEP = len(GEN_STEPS)

        def gen_graph(b):
            return Graph(b, B + b + 1, 0, B // 2 + b + 1, 1)

        def gen_steps(b, h, r):
            for i, slots in enumerate(GEN_STEPS):
                before = sum(len(v) for v in GEN_STEPS[:i])
                yield Step(S0 + b * SG + h * (GR * GSTEP) + r * GSTEP + i,
                           A0 + b * AG + h * (GR * GEN_SLOTS) + r * GEN_SLOTS + before, i % NBANK, h, slots)

        def gen_extraction(b, h, r):
            return B + b * (NH * GR) + h * GR + r + 1

        def gen_sp(b):
            G = gen_graph(b)
            load_adj(G)
            load_xt(G)
            load_x(G)
            store_y(G)

        def gen_pe(b):
            G = gen_graph(b)
            transpose_mask(G)
            rank_product(G)
            table_product(G)
            for h in range(NH):
                with nc.tensor.Fori(0, GR) as r:
                    for T in gen_steps(b, h, r):
                        gather(G, T)
            transpose_agg(G, A0 + (b + 1) * AG)
            update_product(G)

        def gen_act(b):
            G = gen_graph(b)
            copy_mask(G)
            split_bits(G)
            table_hi(G, S0 + b * SG)
            table_mid(G)
            for h in range(NH):
                with nc.scalar.Fori(0, GR) as r:
                    make_weights(G, gen_extraction(b, h, r), A0 + b * AG + (h * GR + r) * GEN_SLOTS)
                    for T in gen_steps(b, h, r):
                        square(T)
                        gelu(T)
            copy_agg_t(G)

        def gen_pool(b):
            G = gen_graph(b)
            make_keys(G, gen_extraction(b, 0, 0) - 1)
            table_rest(G)
            for h in range(NH):
                with nc.gpsimd.Fori(0, GR) as r:
                    for T in gen_steps(b, h, r):
                        rsqrt(T)
                        shift(T)
            rstd_update(G)
            residual(G)
            rstd_out(G)

        def gen_dve(b):
            dve = nc.vector
            G = gen_graph(b)
            make_mask(G)
            make_rank(G)
            make_rest(G)
            for h in range(NH):
                dve.wait_ge(keys_done, G.n)
                wait(dve, aggt_ps, G.n - 1)
                dve.memset(agg[:, 0, h, :], 0.0).then_inc(gen_kept, 1)
                dve.tensor_scalar(slot_no[:, :], slot_i[:, :], 1.0, None, ALU.add).then_inc(gen_slot, 1)
                with dve.Fori(0, GR) as r:
                    t = gen_extraction(b, h, r)
                    done = b * (NH * (GR + 1)) + h * (GR + 1) + r + 1
                    dve.wait_ge(gen_slot, done)
                    dve.wait_ge(gen_kept, done)
                    extract(G, FAST_CAP, t)
                    for T in gen_steps(b, h, r):
                        make_onehot(G, T, slot_ap=True)
                        for q in range(len(T.slots)):
                            norm_slot(T, q)
                        for q in range(len(T.slots)):
                            acc_slot(G, T, q, t)
                    dve.wait_ge(top_done, t)
                    for u in range(2):
                        last = dve.scalar_tensor_tensor(key[:, u, h, :], key[:, u, h, :], top[:, 0, h, u, GEN_SLOTS - 1:GEN_SLOTS],
                                                        key[:, u, h, :], ALU.is_lt, ALU.mult)
                    last.then_inc(gen_kept, 1)
                    dve.tensor_scalar(slot_no[:, :], slot_no[:, :], float(GEN_SLOTS), None, ALU.add).then_inc(gen_slot, 1)
            update_moments(G)
            update_norm(G)
            out_moments(G)
            out_norm(G)

        def general_pass(eng, one_graph, at_end=None):
            eng.wait_ge(flag_done, 1)
            more = eng.value_load(flag[0:1, 0:1], min_val=0, max_val=1)
            with eng.If(more > 0):
                with eng.Fori(0, B) as b:
                    one_graph(b)
                if at_end:
                    at_end()

        block = ctx.enter_context(nc.Block())

        @block.sync
        def _(sp):
            for dst, src in ((w1[:, :, :], W1.rearrange("(a p) o -> p a o", p=P)), (w2[:, :, :], W2.rearrange("(a p) o -> p a o", p=P)),
                             (b1r[:, :], b1.unsqueeze(0)), (b2r[:, :], b2.unsqueeze(0)),
                             (g1b[:, :], g1.partition_broadcast(P)), (be1b[:, :], be1.partition_broadcast(P)),
                             (g2b[:, :], g2.partition_broadcast(P)), (be2b[:, :], be2.partition_broadcast(P))):
                sp.dma_start(dst, src).then_inc(weights_in, 16)
            fast_pass(sp, sp_graph)
            sp.wait_ge(out_written[0], 16 * (B // 2))
            sp.wait_ge(out_written[1], 16 * (B // 2))
            general_pass(sp, gen_sp, lambda: sp.wait_ge(out_written[0], 16 * (B // 2 + B)))

        @block.gpsimd
        def _(pool):
            pool.memset(ones[:, :], 1.0)
            pool.memset(ones_row[:, :], 1.0)
            pool.memset(minus_half[:, :], -0.5)
            pool.memset(eps[:, :], LN_EPS)
            pool.memset(eps_o[:, :], LN_EPS * O)
            pool.memset(over[:, :, :], 0.0)
            pool.memset(ident32[:, :], 0.0)
            pool.memset(ident[:, :], 0.0)
            pool.iota(order_i[:, :, :], pattern=[[0, NH], [-1, N]], base=N - 1, channel_multiplier=0)
            pool.iota(slot_i[:, :], pattern=[[1, GEN_SLOTS]], base=0, channel_multiplier=0).then_inc(consts_pool, 1)
            pool.wait_ge(consts_pool, 1)
            pool.tensor_scalar(order[:, :, :], order_i[:, :, :], 65536.0, 0.0, ALU.mult, ALU.add)
            pool.affine_select(out=ident[:, :], in_=ident[:, :], compare_op=ALU.not_equal, fill=1.0, base=0, pattern=[[-1, P]], channel_multiplier=1)
            pool.affine_select(out=ident32[:, :], in_=ident32[:, :], compare_op=ALU.not_equal, fill=1.0, base=0, pattern=[[-1, P]], channel_multiplier=1)
            pool.affine_select(out=upto[:, :], in_=ones[:, :], compare_op=ALU.is_ge, fill=0.0, base=0, pattern=[[1, P]], channel_multiplier=-1).then_inc(consts_pool, 1)
            pool.wait_ge(consts_pool, 2)
            pool.wait_ge(weights_in, 8 * 16)
            fast_pass(pool, pool_graph)
            general_pass(pool, gen_pool)

        @block.tensor
        def _(pe):
            pe.wait_ge(consts_pool, 2)
            pe.wait_ge(consts_dve, 2)
            pe.wait_ge(weights_in, 8 * 16)
            fast_pass(pe, pe_graph)
            pe.wait_ge(over_red, 1)
            pe.transpose(end_ps[0:1, 0, 0, :], over1[:, :], ident32[:, :]).then_inc(over_t, 1)
            general_pass(pe, gen_pe)

        @block.scalar
        def _(act):
            act.wait_ge(consts_pool, 2)
            fast_pass(act, act_graph)
            general_pass(act, gen_act)

        @block.vector
        def _(dve):
            dve.wait_ge(weights_in, 8 * 16)
            dve.tensor_reduce(w1sum[:, :], w1[:, :, :], AX.X, ALU.add)
            dve.tensor_scalar(g1o[:, :], g1b[:, :], math.sqrt(O), None, ALU.mult)
            dve.tensor_reduce(b1sum[:, :], b1r[:, :], AX.X, ALU.add).then_inc(consts_dve, 1)
            dve.wait_ge(consts_dve, 1)
            dve.scalar_tensor_tensor(w1c[:, :, :], w1sum[:, :].unsqueeze(2).to_broadcast([P, 2, O]), -1.0 / O, w1[:, :, :], ALU.mult, ALU.add)
            dve.scalar_tensor_tensor(b1c[:, :], b1sum[:, :].to_broadcast([1, O]), -1.0 / O, b1r[:, :], ALU.mult, ALU.add).then_inc(consts_dve, 1)
            dve.wait_ge(consts_pool, 2)
            fast_pass(dve, dve_graph)
            dve.wait_ge(over_done, NH * B)
            dve.tensor_reduce(over1[:, :], over[:, :, :].rearrange("p h u -> p (h u)"), AX.X, ALU.max).then_inc(over_red, 1)
            dve.wait_ge(over_t, 1)
            dve.tensor_reduce(over2[:, :], end_ps[0:1, 0, 0, :], AX.X, ALU.max).then_inc(over_max, 1)
            dve.wait_ge(over_max, 1)
            dve.tensor_scalar(flag[:, :], over2[:, :], 0.0, None, ALU.is_gt).then_inc(flag_done, 1)
            general_pass(dve, gen_dve)


_INS = ["x", "adj", "L0_gnn_W1", "L0_gnn_b1", "L0_gnn_g1", "L0_gnn_be1", "L0_gnn_W2", "L0_gnn_b2", "L0_gnn_g2", "L0_gnn_be2"]


def kernel(**inputs):
    import numpy as _np
    import concourse.bacc as _bacc
    from concourse import mybir as _mybir
    from concourse.bass_utils import run_bass_kernel_spmd as _run

    nc = _bacc.Bacc("TRN2", target_bir_lowering=False, num_devices=1)
    arrays, aps = {}, {}
    laid_out = {name: _np.ascontiguousarray(inputs[name]) for name in _INS}
    laid_out["xt"] = _np.ascontiguousarray(_np.transpose(laid_out["x"], (0, 2, 1)))
    for name, a in laid_out.items():
        arrays[f"in_{name}"] = a
        aps[name] = nc.dram_tensor(f"in_{name}", a.shape, _mybir.dt.from_np(a.dtype), kind="ExternalInput").ap()
    out = nc.dram_tensor("out_0", (B, N, O), _mybir.dt.float32, kind="ExternalOutput").ap()
    gnn_kernel(nc, aps["x"], aps["xt"], aps["adj"], *(aps[n] for n in _INS[2:]), out)
    r = _run(nc, [arrays], core_ids=[0])
    return r.results[0]["out_0"]
```

```python
import math
from collections import namedtuple
from contextlib import ExitStack

import concourse.bass as bass
from concourse import mybir

B, N, D, O = 32, 256, 128, 128
P = 128
NH = N // P
LN_EPS = 1e-5

BASE = 8
RICH = 32
RANKS = P // RICH
RICH_SLOTS = 2
CAP = BASE + RANKS * RICH_SLOTS
FAST_STEPS = [(0, (0, 1, 2, 3)), (0, (4, 5, 6, 7)), (1, (0, 1, 2)), (1, (3, 4, 5)), (1, (6, 7)), (NH, (0, 1))]
NBANK = 3
NBUF = len(FAST_STEPS)
GEN_SLOTS = 12
GEN_STEPS = [(0, 1, 2, 3), (4, 5, 6, 7), (8, 9, 10, 11)]
GEN_ROUNDS = -(-N // GEN_SLOTS)
EXTRACTED = 16

Graph = namedtuple("Graph", "b n par m back r")
Step = namedtuple("Step", "s a bank buf back h slots")


def gnn_kernel(nc, x, xt, adj, W1, b1, g1, be1, W2, b2, g2, be2, out):
    fp32, bf16, i32, u16 = mybir.dt.float32, mybir.dt.bfloat16, mybir.dt.int32, mybir.dt.uint16
    ALU, ACT, AX = mybir.AluOpType, mybir.ActivationFunctionType, mybir.AxisListType
    S = len(FAST_STEPS)
    KTOT = sum(len(slots) for _, slots in FAST_STEPS)

    ctx = ExitStack()
    with ctx:
        def sb(name, shape, dt=fp32):
            return ctx.enter_context(nc.sbuf_tensor(name, shape, dt))

        def ps(name, shape, dt=fp32):
            return ctx.enter_context(nc.psum_tensor(name, shape, dt))

        def sem(name):
            return ctx.enter_context(nc.semaphore(name))

        ident = sb("ident", [P, P], bf16)
        minus_ident = sb("minus_ident", [P, P], bf16)
        ident32 = sb("ident32", [P, P])
        upto = sb("upto", [P, P], bf16)
        upto_edge = sb("upto_edge", [P, P], bf16)
        ones = sb("ones", [P, P], bf16)
        ones_row = sb("ones_row", [1, P])
        order = sb("order", [P, NH, N])
        order_i = sb("order_i", [P, NH, N], i32)
        minus_half = sb("minus_half", [P, 4])
        eps = sb("eps", [P, 4])
        eps_o = sb("eps_o", [P, 4])
        slot_no = sb("slot_no", [P, GEN_SLOTS])
        slot_i = sb("slot_i", [P, GEN_SLOTS], i32)
        node_no = sb("node_no", [P, P])
        node_i = sb("node_i", [P, RANKS, RICH], i32)
        rank_no = sb("rank_no", [P, RICH_SLOTS, P], bf16)
        rank_i = sb("rank_i", [P, RICH_SLOTS, RANKS, RICH], i32)
        own_rank = sb("own_rank", [P, RICH_SLOTS])
        w1 = sb("w1", [P, 2, O])
        w1sum = sb("w1sum", [P, 2])
        w1c = sb("w1c", [P, 2, O])
        w2 = sb("w2", [P, 2, O])
        b1r = sb("b1r", [1, O])
        b1sum = sb("b1sum", [1, 1])
        b1c = sb("b1c", [1, NH, 2 * O])
        b2r = sb("b2r", [1, O])
        g1b = sb("g1b", [P, O])
        g1o = sb("g1o", [P, O])
        be1b = sb("be1b", [P, O])
        g2b = sb("g2b", [P, O])
        be2b = sb("be2b", [P, O])

        adj_sb = sb("adj_sb", [P, 2, NH, N])
        xt_sb = sb("xt_sb", [P, 2, N])
        xt_late = sb("xt_late", [P, 2, N])
        x_sb = sb("x_sb", [P, 2, NH, D])
        mask = sb("mask", [P, 2, NH, N], bf16)
        mask_t = sb("mask_t", [P, NH, N], bf16)
        rank_t = sb("rank_t", [P, 2, NH, N], bf16)
        tab = sb("tab", [P, 2, 3, NH, 2 * O], bf16)
        adj_n = sb("adj_n", [P, NH, N])
        halves = sb("halves", [P, 2, NH, N])
        place = sb("place", [P, NH, N])
        key = sb("key", [P, 2, NH, N])
        key2 = sb("key2", [P, NH, 2, N])
        top = sb("top", [P, 2, NH, 2, EXTRACTED])
        top_i = sb("top_i", [P, NH, 2, EXTRACTED], i32)
        wgt = sb("wgt", [P, 2, NH, EXTRACTED])
        agg = sb("agg", [P, 2, NH, O])
        agg_t = sb("agg_t", [P, NH, P])
        over = sb("over", [P, 2, NH])

        rich = sb("rich", [P, NH], bf16)
        rich_at = sb("rich_at", [P, NH])
        sel = sb("sel", [P, 2, NH, P], bf16)
        sel32 = sb("sel32", [P, NH, P])
        sel_t = sb("sel_t", [P, 2, NH, P])
        mask_r = sb("mask_r", [P, NH, P], bf16)
        rank_r = sb("rank_r", [P, NH, P], bf16)
        adj_r = sb("adj_r", [P, N])
        chosen = sb("chosen", [P, 2, RICH_SLOTS, N])
        wgt_r = sb("wgt_r", [P, 2, RICH_SLOTS])
        agg_r = sb("agg_r", [P, O])

        onehot = sb("onehot", [P, NBUF, 4, NH, P], bf16)
        squares = sb("squares", [P, NBUF, 4, O], bf16)
        ssq = sb("ssq", [P, NBUF, 4])
        var1 = sb("var1", [P, NBUF, 4])
        rstd = sb("rstd", [P, NBUF, 4])
        msg = sb("msg", [P, NBUF, 4, O])

        stats = sb("stats", [P, NH, 6])
        moments = sb("moments", [P, NH, 2])
        veps = sb("veps", [P, NH])
        rstd2 = sb("rstd2", [P, NH])
        shift2 = sb("shift2", [P, NH])
        upd = sb("upd", [P, NH, O])
        stats3 = sb("stats3", [P, NH, 6])
        moments3 = sb("moments3", [P, NH, 2])
        veps3 = sb("veps3", [P, NH])
        rstd3 = sb("rstd3", [P, NH])
        shift3 = sb("shift3", [P, NH])
        y = sb("y", [P, 2, NH, O])
        carrier = sb("carrier", [P, 5])
        over_by = sb("over_by", [P, 2, NH])
        over1 = sb("over1", [P, 1])
        over2 = sb("over2", [1, 1])
        flag = sb("flag", [1, 1], i32)

        pre = [ps(f"pre{i}", [P, 4, O]) for i in range(NBANK)]
        rank_ps = ps("rank_ps", [P, NH, N])
        tab_ps = ps("tab_ps", [P, NH, 2 * O])
        end_ps = ps("end_ps", [P, 2, NH, P])
        rich_ps = ps("rich_ps", [P, 2, N])
        small_ps = ps("small_ps", [P, 2 * N])
        mask_ps = small_ps[:, 0:N].bitcast(bf16).rearrange("p (h j) -> p h j", h=NH)
        sel_ps = small_ps[:, N:N + P].bitcast(bf16).rearrange("p (h j) -> p h j", h=NH)
        counts_ps = small_ps[:, N + P:N + P + 2 * NH].rearrange("p (a h) -> p a h", a=2)

        weights_in = sem("weights_in")
        consts_pool = sem("consts_pool")
        consts_dve = sem("consts_dve")
        adj_in = [sem("adj_in0"), sem("adj_in1")]
        xt_in = [sem("xt_in0"), sem("xt_in1")]
        x_in = [sem("x_in0"), sem("x_in1")]
        late_in = [sem("late_in0"), sem("late_in1")]
        mask_done = sem("mask_done")
        maskt_ps = sem("maskt_ps")
        maskt_sb = sem("maskt_sb")
        rank_psd = sem("rank_psd")
        rank_done = sem("rank_done")
        tab_psd = sem("tab_psd")
        hi_done = sem("hi_done")
        less_hi = sem("less_hi")
        mid_done = sem("mid_done")
        less_mid = sem("less_mid")
        tab_done = sem("tab_done")
        adjn_done = sem("adjn_done")
        place_done = sem("place_done")
        halves_done = sem("halves_done")
        keys_done = sem("keys_done")
        top8 = sem("top8")
        cut = sem("cut")
        top_done = sem("top_done")
        topi_done = sem("topi_done")
        wgt_done = sem("wgt_done")
        over_done = sem("over_done")
        deg_psd = sem("deg_psd")
        rich_done = sem("rich_done")
        richat_psd = sem("richat_psd")
        richat_done = sem("richat_done")
        sel_done = sem("sel_done")
        sel32_done = sem("sel32_done")
        selt_psd = sem("selt_psd")
        maskr_psd = sem("maskr_psd")
        adjr_psd = sem("adjr_psd")
        selt_done = sem("selt_done")
        maskr_done = sem("maskr_done")
        adjr_done = sem("adjr_done")
        rankr_psd = sem("rankr_psd")
        rankr_done = sem("rankr_done")
        wgtr_done = sem("wgtr_done")
        onehot_done = sem("onehot_done")
        pre_done = sem("pre_done")
        ssq_done = sem("ssq_done")
        var_done = sem("var_done")
        rstd_done = sem("rstd_done")
        norm_done = sem("norm_done")
        shift_done = sem("shift_done")
        gelu_done = sem("gelu_done")
        acc_done = sem("acc_done")
        aggt_ps = sem("aggt_ps")
        aggt_sb = sem("aggt_sb")
        upd_ps = sem("upd_ps")
        st_done = sem("st_done")
        mom_done = sem("mom_done")
        veps_done = sem("veps_done")
        rstd2_done = sem("rstd2_done")
        shift2_done = sem("shift2_done")
        updn_done = sem("updn_done")
        y_steps = sem("y_steps")
        st3_done = sem("st3_done")
        mom3_done = sem("mom3_done")
        veps3_done = sem("veps3_done")
        rstd3_done = sem("rstd3_done")
        shift3_done = sem("shift3_done")
        y_done = sem("y_done")
        out_written = [sem("out_written0"), sem("out_written1")]
        over_less = sem("over_less")
        over_red = sem("over_red")
        over_t = sem("over_t")
        over_max = sem("over_max")
        flag_done = sem("flag_done")
        gen_kept = sem("gen_kept")
        gen_slot = sem("gen_slot")

        def wait(eng, s, value):
            if not isinstance(value, int) or value > 0:
                eng.wait_ge(s, value)


        def load_adj(G, fast=True):
            wait(nc.sync, mask_done, G.n - G.back)
            wait(nc.sync, adjn_done, G.n - G.back)
            if fast:
                wait(nc.sync, adjr_psd, G.n - G.back)
            nc.sync.dma_start(adj_sb[:, G.par], adj[G.b].rearrange("(h p) j -> p h j", p=P)).then_inc(adj_in[G.par], 16)

        def load_xt(G):
            wait(nc.sync, tab_psd, G.n - G.back)
            nc.sync.dma_start(xt_sb[:, G.par], xt[G.b]).then_inc(xt_in[G.par], 16)

        def load_xt_late(G):
            wait(nc.sync, upd_ps, G.n - G.back)
            nc.sync.dma_start(xt_late[:, G.par], xt[G.b]).then_inc(late_in[G.par], 16)

        def load_x(G):
            wait(nc.sync, y_steps, 3 * (G.n - G.back))
            nc.sync.dma_start(x_sb[:, G.par], x[G.b].rearrange("(h p) d -> p h d", p=P)).then_inc(x_in[G.par], 16)

        def store_y(G):
            nc.sync.wait_ge(y_done, G.n)
            nc.sync.dma_start(out[G.b].rearrange("(h p) o -> p h o", p=P), y[:, G.par]).then_inc(out_written[G.par], 16)

        def transpose_mask(G):
            nc.tensor.wait_ge(mask_done, G.n)
            wait(nc.tensor, maskt_sb, G.n - 1)
            wait(nc.tensor, over_done, G.r)
            for h in range(NH):
                for jb in range(NH):
                    last = nc.tensor.transpose(mask_ps[:, jb, h * P:(h + 1) * P], mask[:, G.par, h, jb * P:(jb + 1) * P], ident[:, :])
            last.then_inc(maskt_ps, 1)

        def rank_product(G):
            nc.tensor.wait_ge(maskt_sb, G.n)
            wait(nc.tensor, rank_done, G.n - 1)
            nc.tensor.matmul(rank_ps[:, 0, :], upto_edge[:, :], mask_t[:, 0, :], start=True, stop=True)
            nc.tensor.matmul(rank_ps[:, 1, :], ones[:, :], mask_t[:, 0, :], start=True, stop=False)
            nc.tensor.matmul(rank_ps[:, 1, :], upto_edge[:, :], mask_t[:, 1, :], start=False, stop=True).then_inc(rank_psd, 1)

        def table_product(G):
            nc.tensor.wait_ge(xt_in[G.par], 16 * G.m)
            wait(nc.tensor, tab_done, G.n - 1)
            nc.tensor.matmul(tab_ps[:, :, :].rearrange("p h o -> p (h o)"), ones_row[:, :],
                             b1c[:, :, :].rearrange("p h o -> p (h o)"), start=True, stop=False, skip_group_check=True)
            for h in range(NH):
                last = nc.tensor.matmul(tab_ps[:, h, :], xt_sb[:, G.par, h * P:(h + 1) * P],
                                        w1c[:, :, :].rearrange("p a o -> p (a o)"), start=False, stop=True, skip_group_check=True)
            last.then_inc(tab_psd, 1)

        def table_less(G, part, taken, done):
            nc.tensor.wait_ge(taken, G.n)
            nc.tensor.matmul(tab_ps[:, :, :].rearrange("p h o -> p (h o)"), minus_ident[:, :],
                             tab[:, G.par, part].rearrange("p h o -> p (h o)"), start=False, stop=True, skip_group_check=True).then_inc(done, 1)

        def degrees(G):
            nc.tensor.wait_ge(maskt_sb, G.n)
            wait(nc.tensor, selt_done, G.r)
            for h in range(NH):
                for jb in range(NH):
                    last = nc.tensor.matmul(counts_ps[:, 0, h:h + 1], mask_t[:, jb, h * P:(h + 1) * P], ones[:, 0:1],
                                            start=(jb == 0), stop=(jb == NH - 1))
            last.then_inc(deg_psd, 1)

        def count_rich(G):
            nc.tensor.wait_ge(rich_done, G.n)
            nc.tensor.matmul(counts_ps[:, 1, 0:1], upto[:, :], rich[:, 0:1], start=True, stop=True)
            nc.tensor.matmul(counts_ps[:, 1, 1:2], ones[:, :], rich[:, 0:1], start=True, stop=False)
            nc.tensor.matmul(counts_ps[:, 1, 1:2], upto[:, :], rich[:, 1:2], start=False, stop=True).then_inc(richat_psd, 1)

        def transpose_sel(G):
            pe = nc.tensor
            pe.wait_ge(sel_done, G.n)
            pe.wait_ge(over_done, G.n)
            for h in range(NH):
                last = pe.transpose(sel_ps[:, h, :], sel[:, G.par, h, :], ident[:, :])
            last.then_inc(selt_psd, 1)

        def rich_products(G):
            pe = nc.tensor
            wait(pe, rankr_done, G.n - 1)
            wait(pe, wgtr_done, G.n - 1)
            for jb in range(NH):
                for h in range(NH):
                    last = pe.matmul(rich_ps[:, 0, jb * P:(jb + 1) * P], mask[:, G.par, h, jb * P:(jb + 1) * P], sel[:, G.par, h, :],
                                     start=(h == 0), stop=(h == NH - 1))
            last.then_inc(maskr_psd, 1)
            pe.wait_ge(sel32_done, G.n)
            for h in range(NH):
                last = pe.matmul(rich_ps[:, 1, :], sel32[:, h, :], adj_sb[:, G.par, h, :], start=(h == 0), stop=(h == NH - 1))
            last.then_inc(adjr_psd, 1)

        def rich_rank_products(G):
            pe = nc.tensor
            pe.wait_ge(maskr_done, G.n)
            pe.wait_ge(adjr_done, G.n)
            pe.matmul(rich_ps[:, 0, 0:P], upto_edge[:, :], mask_r[:, 0, :], start=True, stop=True)
            pe.matmul(rich_ps[:, 0, P:N], ones[:, :], mask_r[:, 0, :], start=True, stop=False)
            pe.matmul(rich_ps[:, 0, P:N], upto_edge[:, :], mask_r[:, 1, :], start=False, stop=True)
            pe.matmul(rich_ps[:, 1, 0:P], mask_r[:, 0, :], upto_edge[:, :], start=True, stop=True)
            pe.matmul(rich_ps[:, 1, P:N], mask_r[:, 0, :], ones[:, :], start=True, stop=False)
            pe.matmul(rich_ps[:, 1, P:N], mask_r[:, 1, :], upto_edge[:, :], start=False, stop=True).then_inc(rankr_psd, 1)

        def gather(G, T):
            nc.tensor.wait_ge(onehot_done, T.s + 1)
            nc.tensor.wait_ge(tab_done, G.n)
            wait(nc.tensor, norm_done, T.s - NBANK + 1)
            kn = len(T.slots)
            own = [(sel[:, G.par, h, :], h) for h in range(NH)] if T.h == NH else [(ident[:, :], T.h)]
            for a, (pick, h) in enumerate(own):
                for part in range(3):
                    nc.tensor.matmul(pre[T.bank][:, 0:kn, :], pick,
                                     tab[:, G.par, part, h, O:2 * O].unsqueeze(1).to_broadcast([P, kn, O]),
                                     start=(a == 0 and part == 0), stop=False, skip_group_check=True)
            for q in range(kn):
                for jb in range(NH):
                    for part in range(3):
                        last = nc.tensor.matmul(pre[T.bank][:, q, :], onehot[:, T.buf, q, jb, :],
                                                tab[:, G.par, part, jb, 0:O], start=False,
                                                stop=(jb == NH - 1 and part == 2), skip_group_check=True)
            last.then_inc(pre_done, 1)

        def transpose_agg(G, a_end, fast=True):
            nc.tensor.wait_ge(acc_done, a_end)
            wait(nc.tensor, updn_done, G.n - 1)
            if fast:
                nc.tensor.wait_ge(selt_done, G.n)
                nc.tensor.matmul(end_ps[:, 0, :, :], agg_r[:, :], sel_t[:, G.par], start=True, stop=False, skip_group_check=True)
            for h in range(NH):
                last = nc.tensor.matmul(end_ps[:, 0, h, :], agg[:, G.par, h, :], ident32[:, :], start=not fast, stop=True, skip_group_check=True)
            last.then_inc(aggt_ps, 1)

        def update_product(G):
            nc.tensor.wait_ge(aggt_sb, G.n)
            nc.tensor.wait_ge(late_in[G.par], 16 * G.m)
            for h in range(NH):
                nc.tensor.matmul(end_ps[:, 1, h, :], xt_late[:, G.par, h * P:(h + 1) * P], w2[:, 0, :], start=True, stop=False)
                nc.tensor.matmul(end_ps[:, 1, h, :], agg_t[:, h, :], w2[:, 1, :], start=False, stop=False)
                last = nc.tensor.matmul(end_ps[:, 1, h, :], ones_row[:, :], b2r[:, :], start=False, stop=True)
            last.then_inc(upd_ps, 1)

        def copy_mask(G, mask_free):
            nc.scalar.wait_ge(maskt_ps, G.n)
            wait(nc.scalar, rank_psd, G.n - 1)
            wait(nc.scalar, deg_psd, mask_free)
            nc.scalar.copy(mask_t[:, :, :], mask_ps[:, :, :]).then_inc(maskt_sb, 1)

        def copy_rank(G, s_free):
            nc.scalar.wait_ge(rank_psd, G.n)
            wait(nc.scalar, onehot_done, s_free)
            nc.scalar.copy(rank_t[:, G.par], rank_ps[:, :, :]).then_inc(rank_done, 1)

        def copy_rich_rank(G):
            nc.scalar.wait_ge(rankr_psd, G.n)
            wait(nc.scalar, onehot_done, S * (G.n - 1))
            nc.scalar.copy(rank_r[:, :, :], rich_ps[:, 0, :].rearrange("p (h j) -> p h j", h=NH)).then_inc(rankr_done, 1)

        def plus_zero(G):
            nc.scalar.wait_ge(adj_in[G.par], 16 * G.m)
            wait(nc.scalar, halves_done, 2 * (G.n - 1))
            nc.scalar.activation(adj_n[:, :, :], adj_sb[:, G.par], ACT.Identity).then_inc(adjn_done, 1)

        def split_bits(G, half):
            nc.scalar.wait_ge(adjn_done, G.n)
            wait(nc.scalar, keys_done, 2 * G.n - 3 + half)
            bits = adj_n[:, :, :].bitcast(u16).rearrange("p h (j t) -> p t h j", t=2)
            nc.scalar.copy(halves[:, half], bits[:, half]).then_inc(halves_done, 1)

        def copy_sel(G):
            nc.scalar.wait_ge(sel_done, G.n)
            wait(nc.scalar, adjr_psd, G.n - 1)
            nc.scalar.copy(sel32[:, :, :], sel[:, G.par]).then_inc(sel32_done, 1)

        def copy_rich(G):
            act = nc.scalar
            act.wait_ge(adjr_psd, G.n)
            wait(act, rankr_psd, G.n - 1)
            act.copy(mask_r[:, :, :], rich_ps[:, 0, :].rearrange("p (h j) -> p h j", h=NH)).then_inc(maskr_done, 1)
            wait(act, wgtr_done, G.n - 1)
            act.copy(adj_r[:, :], rich_ps[:, 1, :]).then_inc(adjr_done, 1)

        def copy_sel_t(G):
            act = nc.scalar
            act.wait_ge(selt_psd, G.n)
            wait(act, aggt_ps, G.n - 2)
            act.copy(sel_t[:, G.par], sel_ps[:, :, :]).then_inc(selt_done, 1)

        def table_hi(G, s_free):
            nc.scalar.wait_ge(tab_psd, G.n)
            wait(nc.scalar, pre_done, s_free)
            nc.scalar.copy(tab[:, G.par, 0], tab_ps[:, :, :]).then_inc(hi_done, 1)

        def table_rest(G, part, left, done):
            nc.scalar.wait_ge(left, G.n)
            nc.scalar.copy(tab[:, G.par, part], tab_ps[:, :, :]).then_inc(done, 1)

        def square(T):
            nc.scalar.wait_ge(pre_done, T.s + 1)
            wait(nc.scalar, rstd_done, T.s - T.back + 1)
            for q in range(len(T.slots)):
                last = nc.scalar.activation(squares[:, T.buf, q, :], pre[T.bank][:, q, :], ACT.Square, accum_out=ssq[:, T.buf, q:q + 1])
            last.then_inc(ssq_done, 1)
            nc.scalar.wait_ge(ssq_done, T.s + 1)
            kn = len(T.slots)
            nc.scalar.activation(var1[:, T.buf, 0:kn], ssq[:, T.buf, 0:kn], ACT.Identity, bias=eps_o[:, 0:1]).then_inc(var_done, 1)

        def gelu(T):
            nc.scalar.wait_ge(shift_done, T.s + 1)
            kn = len(T.slots)
            nc.scalar.activation(msg[:, T.buf, 0:kn, :], msg[:, T.buf, 0:kn, :], ACT.Gelu).then_inc(gelu_done, 1)

        def make_weights(G, t, wgt_free, width):
            act = nc.scalar
            act.wait_ge(top_done, t)
            wait(act, wgt_done, t - 1)
            wait(act, acc_done, wgt_free)
            act.copy(top_i[:, :, :, 0:width], top[:, G.par, :, :, 0:width]).then_inc(topi_done, 1)
            act.wait_ge(topi_done, t)
            low = top_i[:, :, :, 0:width].bitcast(u16).rearrange("p h t (k u) -> p u t h k", u=2)
            to = wgt[:, G.par, :, 0:width].bitcast(u16).rearrange("p h (k u) -> p u h k", u=2)
            act.copy(to[:, 1], low[:, 0, 0])
            act.copy(to[:, 0], low[:, 0, 1]).then_inc(wgt_done, 1)

        def copy_agg_t(G):
            nc.scalar.wait_ge(aggt_ps, G.n)
            wait(nc.scalar, upd_ps, G.n - 1)
            nc.scalar.copy(agg_t[:, :, :], end_ps[:, 0]).then_inc(aggt_sb, 1)

        def update_norm(G):
            act = nc.scalar
            act.wait_ge(shift2_done, G.n)
            wait(act, y_steps, 3 * (G.n - 1))
            for h in range(NH):
                last = act.activation(upd[:, h, :], end_ps[:, 1, h, :], ACT.Identity, bias=shift2[:, h:h + 1], scale=rstd2[:, h:h + 1])
            last.then_inc(updn_done, 1)

        def out_norm(G):
            act = nc.scalar
            act.wait_ge(shift3_done, G.n)
            for h in range(NH):
                last = act.activation(y[:, G.par, h, :], y[:, G.par, h, :], ACT.Identity, bias=shift3[:, h:h + 1], scale=rstd3[:, h:h + 1])
            last.then_inc(y_done, 1)

        def make_key(G, half, top_free):
            pool = nc.gpsimd
            pool.wait_ge(place_done, G.n)
            wait(pool, top_done, top_free)
            pool.wait_ge(halves_done, 2 * (G.n - 1) + 1 + half)
            pool.tensor_tensor(key[:, 1 - half], place[:, :, :], halves[:, half], ALU.add).then_inc(keys_done, 1)

        def rsqrt(T):
            pool = nc.gpsimd
            kn = len(T.slots)
            pool.wait_ge(var_done, T.s + 1)
            wait(pool, norm_done, T.s - T.back + 1)
            pool.tensor_tensor(rstd[:, T.buf, 0:kn], var1[:, T.buf, 0:kn], minus_half[:, 0:kn], ALU.pow).then_inc(rstd_done, 1)

        def shift(T):
            pool = nc.gpsimd
            kn = len(T.slots)
            pool.wait_ge(norm_done, T.s + 1)
            m = msg[:, T.buf, 0:kn, :]
            pool.tensor_tensor(m, m, be1b[:, :].unsqueeze(1).to_broadcast([P, kn, O]), ALU.add).then_inc(shift_done, 1)

        def rstd_update(G):
            pool = nc.gpsimd
            pool.wait_ge(mom_done, G.n)
            pool.tensor_tensor(veps[:, :], moments[:, :, 1], eps[:, 0:NH], ALU.add).then_inc(veps_done, 1)
            pool.wait_ge(veps_done, G.n)
            wait(pool, updn_done, G.n - 1)
            pool.tensor_tensor(rstd2[:, :], veps[:, :], minus_half[:, 0:NH], ALU.pow).then_inc(rstd2_done, 1)

        def residual(G):
            pool = nc.gpsimd
            def wide(v):
                return v[:, :].unsqueeze(1).to_broadcast([P, NH, O])
            pool.wait_ge(updn_done, G.n)
            wait(pool, out_written[G.par], 16 * (G.m - 1))
            pool.tensor_tensor(y[:, G.par], upd[:, :, :], wide(g2b), ALU.mult).then_inc(y_steps, 1)
            pool.wait_ge(y_steps, 3 * G.n - 2)
            pool.tensor_tensor(y[:, G.par], y[:, G.par], wide(be2b), ALU.add).then_inc(y_steps, 1)
            pool.wait_ge(y_steps, 3 * G.n - 1)
            pool.wait_ge(x_in[G.par], 16 * G.m)
            pool.tensor_tensor(y[:, G.par], y[:, G.par], x_sb[:, G.par], ALU.add).then_inc(y_steps, 1)

        def rstd_out(G):
            pool = nc.gpsimd
            pool.wait_ge(mom3_done, G.n)
            pool.tensor_tensor(veps3[:, :], moments3[:, :, 1], eps[:, 0:NH], ALU.add).then_inc(veps3_done, 1)
            pool.wait_ge(veps3_done, G.n)
            wait(pool, y_done, G.n - 1)
            pool.tensor_tensor(rstd3[:, :], veps3[:, :], minus_half[:, 0:NH], ALU.pow).then_inc(rstd3_done, 1)

        def make_mask(G, rich_free):
            dve = nc.vector
            dve.wait_ge(adj_in[G.par], 16 * G.m)
            wait(dve, maskt_ps, G.n - G.back)
            wait(dve, place_done, G.n - G.back)
            wait(dve, maskr_psd, rich_free)
            dve.tensor_scalar(mask[:, G.par], adj_sb[:, G.par], 0.0, None, ALU.not_equal).then_inc(mask_done, 1)

        def make_places(G):
            dve = nc.vector
            dve.wait_ge(mask_done, G.n)
            wait(dve, keys_done, 2 * (G.n - 1))
            dve.tensor_tensor(place[:, :, :], mask[:, G.par], order[:, :, :], ALU.mult).then_inc(place_done, 1)

        def extract(G, t):
            dve = nc.vector
            dve.wait_ge(keys_done, 2 * G.n)
            wait(dve, topi_done, t - 1)
            dve.memset(carrier[:, 0:1], 0.0)
            for h in range(NH):
                for u in range(2):
                    last = dve.max(top[:, G.par, h, u, 0:8], key[:, u, h, :])
            return last

        def extract_first(G, t):
            extract(G, t).then_inc(top_done, 1)

        def extract_more(G, t):
            dve = nc.vector
            extract(G, t).then_inc(top8, 1)
            dve.wait_ge(top8, t - B)
            for h in range(NH):
                wait(dve, top_done, t - 1)
                for u in range(2):
                    last = dve.scalar_tensor_tensor(key2[:, h, u, :], key[:, u, h, :], top[:, G.par, h, u, 7:8], key[:, u, h, :],
                                                    ALU.is_lt, ALU.mult)
                last.then_inc(cut, 1)
                dve.wait_ge(cut, NH * (t - B - 1) + h + 1)
                dve.memset(carrier[:, 1 + h:2 + h], 0.0)
                for u in range(2):
                    last = dve.max(top[:, G.par, h, u, 8:16], key2[:, h, u, :])
            last.then_inc(top_done, 1)

        def find_rich(G):
            dve = nc.vector
            dve.wait_ge(deg_psd, G.n)
            wait(dve, richat_psd, G.n - 1)
            wait(dve, richat_done, G.n - 1)
            dve.tensor_scalar(rich[:, :], counts_ps[:, 0, :], float(BASE), None, ALU.is_gt).then_inc(rich_done, 1)

        def number_rich(G):
            dve = nc.vector
            dve.wait_ge(richat_psd, G.n)
            wait(dve, sel_done, G.n - 1)
            dve.tensor_tensor(rich_at[:, :], counts_ps[:, 1, :], rich[:, :], ALU.mult).then_inc(richat_done, 1)
            wait(dve, over_done, G.n - 1)
            dve.tensor_tensor(over[:, :, :], over[:, :, :], counts_ps[:, :, :], ALU.max).then_inc(over_done, 1)

        def select_rich(G, s_free):
            dve = nc.vector
            dve.wait_ge(richat_done, G.n)
            wait(dve, sel32_done, G.n - 2)
            wait(dve, pre_done, s_free)
            for h in range(NH):
                last = dve.tensor_scalar(sel[:, G.par, h, :], node_no[:, :], rich_at[:, h:h + 1], None, ALU.is_equal)
            last.then_inc(sel_done, 1)

        def rich_weights(G, a_free):
            dve = nc.vector
            dve.wait_ge(adjr_done, G.n)
            dve.wait_ge(rankr_done, G.n)
            wait(dve, acc_done, a_free)
            for q in range(RICH_SLOTS):
                last = dve.scalar_tensor_tensor(chosen[:, G.par, q, :], rich_ps[:, 1, :], own_rank[:, q:q + 1], adj_r[:, :],
                                                ALU.is_equal, ALU.mult, accum_out=wgt_r[:, G.par, q:q + 1])
            last.then_inc(wgtr_done, 1)

        def make_onehot(G, T, slot_ap=False):
            dve = nc.vector
            dve.wait_ge(rank_done, G.n)
            wait(dve, pre_done, T.s - T.back + 1)
            if T.h == NH:
                dve.wait_ge(rankr_done, G.n)
                kn = len(T.slots)
                dve.tensor_tensor(onehot[:, T.buf, 0:kn], rank_r[:, :, :].unsqueeze(1).to_broadcast([P, kn, NH, P]),
                                  rank_no[:, :, :].unsqueeze(2).to_broadcast([P, kn, NH, P]), ALU.is_equal).then_inc(onehot_done, 1)
                return
            for q, k in enumerate(T.slots):
                value = slot_no[:, k:k + 1] if slot_ap else float(k - N)
                last = dve.tensor_scalar(onehot[:, T.buf, q], rank_t[:, G.par, :, T.h * P:(T.h + 1) * P], value, None, ALU.is_equal)
            last.then_inc(onehot_done, 1)

        def norm_slot(T, q):
            dve = nc.vector
            if q == 0:
                dve.wait_ge(rstd_done, T.s + 1)
            ins = dve.scalar_tensor_tensor(msg[:, T.buf, q, :], pre[T.bank][:, q, :], rstd[:, T.buf, q:q + 1], g1o[:, :], ALU.mult, ALU.mult)
            if q == len(T.slots) - 1:
                ins.then_inc(norm_done, 1)

        def acc_slot(G, T, q, t, agg_free=None):
            dve = nc.vector
            is_rich = T.h == NH
            if q == 0:
                dve.wait_ge(gelu_done, T.s + 1)
                if is_rich:
                    dve.wait_ge(wgtr_done, G.n)
                else:
                    dve.wait_ge(wgt_done, t)
            first = agg_free is not None and T.slots[q] == 0
            if first:
                wait(dve, aggt_ps, agg_free)
            else:
                dve.wait_ge(acc_done, T.a + q)
            k = T.slots[q]
            a = agg_r[:, :] if is_rich else agg[:, G.par, T.h, :]
            w = wgt_r[:, G.par, k:k + 1] if is_rich else wgt[:, G.par, T.h, k:k + 1]
            if first:
                ins = dve.tensor_scalar(a, msg[:, T.buf, q, :], w, None, ALU.mult)
            else:
                ins = dve.scalar_tensor_tensor(a, msg[:, T.buf, q, :], w, a, ALU.mult, ALU.add)
            ins.then_inc(acc_done, 1)

        def update_moments(G):
            dve = nc.vector
            dve.wait_ge(upd_ps, G.n)
            for h in range(NH):
                last = dve.bn_stats(stats[:, h, :], end_ps[:, 1, h, :])
            last.then_inc(st_done, 1)
            dve.wait_ge(st_done, G.n)
            wait(dve, veps_done, G.n - 1)
            dve.memset(carrier[:, 3:4], 0.0)
            for h in range(NH):
                last = dve.bn_aggr(moments[:, h, :], stats[:, h, :])
            last.then_inc(mom_done, 1)

        def update_shift(G):
            dve = nc.vector
            dve.wait_ge(rstd2_done, G.n)
            wait(dve, updn_done, G.n - 1)
            dve.scalar_tensor_tensor(shift2[:, :], moments[:, :, 0], -1.0, rstd2[:, :], ALU.mult, ALU.mult).then_inc(shift2_done, 1)

        def out_moments(G):
            dve = nc.vector
            dve.wait_ge(y_steps, 3 * G.n)
            for h in range(NH):
                last = dve.bn_stats(stats3[:, h, :], y[:, G.par, h, :])
            last.then_inc(st3_done, 1)
            dve.wait_ge(st3_done, G.n)
            wait(dve, veps3_done, G.n - 1)
            dve.memset(carrier[:, 4:5], 0.0)
            for h in range(NH):
                last = dve.bn_aggr(moments3[:, h, :], stats3[:, h, :])
            last.then_inc(mom3_done, 1)

        def out_shift(G):
            dve = nc.vector
            dve.wait_ge(rstd3_done, G.n)
            wait(dve, y_done, G.n - 1)
            dve.scalar_tensor_tensor(shift3[:, :], moments3[:, :, 0], -1.0, rstd3[:, :], ALU.mult, ALU.mult).then_inc(shift3_done, 1)


        def graph(g, c):
            return Graph(2 * g + c, 2 * g + c + 1, c % 2, g + c // 2 + 1, 2, 2 * g + c)

        def step(g, c, i):
            c, i = c + i // S, i % S
            h, slots = FAST_STEPS[i]
            before = sum(len(v) for _, v in FAST_STEPS[:i])
            return graph(g, c), Step((2 * g + c) * S + i, (2 * g + c) * KTOT + before, i % NBANK, i, NBUF, h, slots)

        def there(g, c, i=0):
            return not isinstance(g, int) or 0 <= 2 * g + c + i // S < B

        def sp_graph(g, c):
            if there(g, c + 2):
                load_xt(graph(g, c + 2))
            if there(g, c):
                load_xt_late(graph(g, c))
            if there(g, c + 2):
                load_adj(graph(g, c + 2))
            if there(g, c):
                load_x(graph(g, c))
            if there(g, c - 2):
                store_y(graph(g, c - 2))

        def pe_graph(g, c):
            for i in range(S):
                if there(g, c):
                    gather(*step(g, c, i))
                if i == 0 and there(g, c + 1):
                    table_product(graph(g, c + 1))
                if i == 1 and there(g, c):
                    transpose_sel(graph(g, c))
                if i == 1 and there(g, c + 1):
                    transpose_mask(graph(g, c + 1))
                if i == 1 and there(g, c):
                    rich_products(graph(g, c))
                if i == 2 and there(g, c + 1):
                    table_less(graph(g, c + 1), 0, hi_done, less_hi)
                    rank_product(graph(g, c + 1))
                    degrees(graph(g, c + 1))
                if i == 3 and there(g, c):
                    rich_rank_products(graph(g, c))
                if i == 3 and there(g, c + 1):
                    table_less(graph(g, c + 1), 1, mid_done, less_mid)
                if i == 3 and there(g, c - 1):
                    transpose_agg(graph(g, c - 1), (2 * g + c) * KTOT)
                if i == 4 and there(g, c + 1):
                    count_rich(graph(g, c + 1))
                if i == 4 and there(g, c - 1):
                    update_product(graph(g, c - 1))

        def act_graph(g, c):
            for i in range(S):
                if there(g, c, i):
                    square(step(g, c, i)[1])
                if there(g, c, i - 2):
                    gelu(step(g, c, i - 2)[1])
                if i == 0 and there(g, c):
                    copy_sel(graph(g, c))
                if i == 0 and there(g, c + 1):
                    table_hi(graph(g, c + 1), S * (2 * g + c))
                if i == 1 and there(g, c + 1):
                    copy_mask(graph(g, c + 1), 2 * g + c + 1)
                if i == 1 and there(g, c):
                    copy_sel_t(graph(g, c))
                    make_weights(graph(g, c), 2 * g + c + 1, KTOT * (2 * g + c - 1), BASE)
                if i == 1 and there(g, c - 2):
                    update_norm(graph(g, c - 2))
                if i == 2 and there(g, c):
                    copy_rich(graph(g, c))
                if i == 2 and there(g, c + 1):
                    table_rest(graph(g, c + 1), 1, less_hi, mid_done)
                    copy_rank(graph(g, c + 1), S * (2 * g + c))
                    plus_zero(graph(g, c + 1))
                if i == 3 and there(g, c):
                    copy_rich_rank(graph(g, c))
                if i == 3 and there(g, c + 1):
                    table_rest(graph(g, c + 1), 2, less_mid, tab_done)
                    split_bits(graph(g, c + 1), 0)
                if i == 3 and there(g, c - 1):
                    copy_agg_t(graph(g, c - 1))
                if i == 4 and there(g, c + 1):
                    split_bits(graph(g, c + 1), 1)
                if i == 5 and there(g, c - 2):
                    out_norm(graph(g, c - 2))

        def pool_graph(g, c):
            for i in range(S):
                if there(g, c, i):
                    rsqrt(step(g, c, i)[1])
                if there(g, c, i - 1):
                    shift(step(g, c, i - 1)[1])
                if i == 2 and there(g, c - 2):
                    residual(graph(g, c - 2))
                if i == 4 and there(g, c - 2):
                    rstd_out(graph(g, c - 2))
                if i == 4 and there(g, c + 1):
                    make_key(graph(g, c + 1), 0, 2 * g + c + 1)
                if i == 5 and there(g, c + 1):
                    make_key(graph(g, c + 1), 1, 2 * g + c + 1)
                if i == 5 and there(g, c - 1):
                    rstd_update(graph(g, c - 1))

        def dve_graph(g, c):
            for i in range(S):
                for ahead in ((1, 2) if i == S - 2 else () if i == S - 3 else (2,)):
                    if there(g, c, i + ahead):
                        make_onehot(*step(g, c, i + ahead))
                norms = [lambda q=q: norm_slot(step(g, c, i - 1)[1], q) for q in range(len(step(g, c, i - 1)[1].slots))] if there(g, c, i - 1) else []
                G, T = step(g, c, i - 3)
                accs = [lambda q=q: acc_slot(G, T, q, G.n, G.n - 1 if T.h == NH else G.n - 2) for q in range(len(T.slots))] if there(g, c, i - 3) else []
                for q in range(4):
                    for ops in (norms, accs):
                        if q < len(ops):
                            ops[q]()
                if i == 0 and there(g, c):
                    extract_first(graph(g, c), 2 * g + c + 1)
                if i == 0 and there(g, c - 2):
                    update_shift(graph(g, c - 2))
                if i == 1 and there(g, c + 1):
                    make_places(graph(g, c + 1))
                if i == 3 and there(g, c - 2):
                    out_moments(graph(g, c - 2))
                if i == 3 and there(g, c + 1):
                    find_rich(graph(g, c + 1))
                if i == 3 and there(g, c):
                    rich_weights(graph(g, c), KTOT * (2 * g + c - 1))
                if i == 5 and there(g, c - 2):
                    out_shift(graph(g, c - 2))
                if i == 5 and there(g, c + 1):
                    number_rich(graph(g, c + 1))
                    select_rich(graph(g, c + 1), S * (2 * g + c))
                if i == 5 and there(g, c + 2):
                    make_mask(graph(g, c + 2), 2 * g + c + 1)
                if i == S - 1 and there(g, c - 1):
                    update_moments(graph(g, c - 1))

        def fast_pass(eng, one_graph):
            for c in (-2, -1, 0, 1):
                one_graph(0, c)
            with eng.Fori(1, B // 2 - 1) as g:
                one_graph(g, 0)
                one_graph(g, 1)
            for c in range(4):
                one_graph(B // 2 - 1, c)


        GR = GEN_ROUNDS
        A0 = B * KTOT
        S0 = B * S
        SG = NH * GR * len(GEN_STEPS)
        AG = NH * GR * GEN_SLOTS
        GSTEP = len(GEN_STEPS)

        def gen_graph(b):
            return Graph(b, B + b + 1, 0, B // 2 + b + 1, 1, B)

        def gen_steps(b, h, r):
            for i, slots in enumerate(GEN_STEPS):
                before = sum(len(v) for v in GEN_STEPS[:i])
                yield Step(S0 + b * SG + h * (GR * GSTEP) + r * GSTEP + i,
                           A0 + b * AG + h * (GR * GEN_SLOTS) + r * GEN_SLOTS + before, i, i, NBANK, h, slots)

        def gen_extraction(b, h, r):
            return B + b * (NH * GR) + h * GR + r + 1

        def gen_sp(b):
            G = gen_graph(b)
            load_adj(G, fast=False)
            load_xt(G)
            load_xt_late(G)
            load_x(G)
            store_y(G)

        def gen_pe(b):
            G = gen_graph(b)
            transpose_mask(G)
            rank_product(G)
            table_product(G)
            table_less(G, 0, hi_done, less_hi)
            table_less(G, 1, mid_done, less_mid)
            for h in range(NH):
                with nc.tensor.Fori(0, GR) as r:
                    for T in gen_steps(b, h, r):
                        gather(G, T)
            transpose_agg(G, A0 + (b + 1) * AG, fast=False)
            update_product(G)

        def gen_act(b):
            G = gen_graph(b)
            copy_mask(G, B)
            copy_rank(G, S0 + b * SG)
            plus_zero(G)
            split_bits(G, 0)
            split_bits(G, 1)
            table_hi(G, S0 + b * SG)
            table_rest(G, 1, less_hi, mid_done)
            table_rest(G, 2, less_mid, tab_done)
            for h in range(NH):
                with nc.scalar.Fori(0, GR) as r:
                    make_weights(G, gen_extraction(b, h, r), A0 + b * AG + (h * GR + r) * GEN_SLOTS, EXTRACTED)
                    for T in gen_steps(b, h, r):
                        square(T)
                        gelu(T)
            copy_agg_t(G)
            update_norm(G)
            out_norm(G)

        def gen_pool(b):
            G = gen_graph(b)
            make_key(G, 0, gen_extraction(b, 0, 0) - 1)
            make_key(G, 1, gen_extraction(b, 0, 0) - 1)
            for h in range(NH):
                with nc.gpsimd.Fori(0, GR) as r:
                    for T in gen_steps(b, h, r):
                        rsqrt(T)
                        shift(T)
            rstd_update(G)
            residual(G)
            rstd_out(G)

        def gen_dve(b):
            dve = nc.vector
            G = gen_graph(b)
            make_mask(G, B)
            make_places(G)
            for h in range(NH):
                dve.wait_ge(gen_slot, b * (NH * (GR + 1)) + h * (GR + 1))
                wait(dve, aggt_ps, G.n - 1)
                dve.memset(agg[:, 0, h, :], 0.0).then_inc(gen_kept, 1)
                dve.tensor_scalar(slot_no[:, :], slot_i[:, :], float(-N), None, ALU.add).then_inc(gen_slot, 1)
                with dve.Fori(0, GR) as r:
                    t = gen_extraction(b, h, r)
                    done = b * (NH * (GR + 1)) + h * (GR + 1) + r + 1
                    dve.wait_ge(gen_slot, done)
                    dve.wait_ge(gen_kept, done)
                    extract_more(G, t)
                    for T in gen_steps(b, h, r):
                        make_onehot(G, T, slot_ap=True)
                        for q in range(len(T.slots)):
                            norm_slot(T, q)
                        for q in range(len(T.slots)):
                            acc_slot(G, T, q, t)
                    dve.wait_ge(top_done, t)
                    for u in range(2):
                        last = dve.scalar_tensor_tensor(key[:, u, h, :], key[:, u, h, :], top[:, 0, h, u, GEN_SLOTS - 1:GEN_SLOTS],
                                                        key[:, u, h, :], ALU.is_lt, ALU.mult)
                    last.then_inc(gen_kept, 1)
                    dve.tensor_scalar(slot_no[:, :], slot_no[:, :], float(GEN_SLOTS), None, ALU.add).then_inc(gen_slot, 1)
            update_moments(G)
            update_shift(G)
            out_moments(G)
            out_shift(G)

        def general_pass(eng, one_graph, at_end=None):
            eng.wait_ge(flag_done, 1)
            more = eng.value_load(flag[0:1, 0:1], min_val=0, max_val=1)
            with eng.If(more > 0):
                with eng.Fori(0, B) as b:
                    one_graph(b)
                if at_end:
                    at_end()

        block = ctx.enter_context(nc.Block())

        @block.sync
        def _(sp):
            for dst, src in ((w1[:, :, :], W1.rearrange("(a p) o -> p a o", p=P)), (w2[:, :, :], W2.rearrange("(a p) o -> p a o", p=P)),
                             (b1r[:, :], b1.unsqueeze(0)), (b2r[:, :], b2.unsqueeze(0)),
                             (g1b[:, :], g1.partition_broadcast(P)), (be1b[:, :], be1.partition_broadcast(P)),
                             (g2b[:, :], g2.partition_broadcast(P)), (be2b[:, :], be2.partition_broadcast(P))):
                sp.dma_start(dst, src).then_inc(weights_in, 16)
            fast_pass(sp, sp_graph)
            sp.wait_ge(out_written[0], 16 * (B // 2))
            sp.wait_ge(out_written[1], 16 * (B // 2))
            general_pass(sp, gen_sp, lambda: sp.wait_ge(out_written[0], 16 * (B // 2 + B)))

        @block.gpsimd
        def _(pool):
            pool.memset(ones[:, :], 1.0)
            pool.memset(ones_row[:, :], 1.0)
            pool.memset(minus_half[:, :], -0.5)
            pool.memset(eps[:, :], LN_EPS)
            pool.memset(eps_o[:, :], LN_EPS * O)
            pool.memset(over[:, :, :], 0.0)
            pool.memset(ident32[:, :], 0.0)
            pool.memset(ident[:, :], 0.0)
            pool.memset(minus_ident[:, :], 0.0)
            pool.iota(order_i[:, :, :], pattern=[[0, NH], [-1, N]], base=N - 1, channel_multiplier=0)
            pool.iota(node_i[:, :, :], pattern=[[0, RANKS], [1, RICH]], base=1, channel_multiplier=0)
            pool.iota(rank_i[:, :, :, :], pattern=[[RANKS, RICH_SLOTS], [1, RANKS], [0, RICH]], base=BASE - N, channel_multiplier=0)
            pool.iota(slot_i[:, :], pattern=[[1, GEN_SLOTS]], base=0, channel_multiplier=0).then_inc(consts_pool, 1)
            pool.wait_ge(consts_pool, 1)
            pool.tensor_scalar(order[:, :, :], order_i[:, :, :], 65536.0, 0.0, ALU.mult, ALU.add)
            pool.affine_select(out=ident[:, :], in_=ident[:, :], compare_op=ALU.not_equal, fill=1.0, base=0, pattern=[[-1, P]], channel_multiplier=1)
            pool.affine_select(out=minus_ident[:, :], in_=minus_ident[:, :], compare_op=ALU.not_equal, fill=-1.0, base=0, pattern=[[-1, P]], channel_multiplier=1)
            pool.affine_select(out=ident32[:, :], in_=ident32[:, :], compare_op=ALU.not_equal, fill=1.0, base=0, pattern=[[-1, P]], channel_multiplier=1)
            pool.affine_select(out=upto[:, :], in_=ones[:, :], compare_op=ALU.is_ge, fill=0.0, base=0, pattern=[[1, P]], channel_multiplier=-1).then_inc(consts_pool, 1)
            pool.wait_ge(consts_pool, 2)
            pool.affine_select(out=upto_edge[:, :], in_=upto[:, :], compare_op=ALU.not_equal, fill=float(-N), base=0, pattern=[[-1, P]], channel_multiplier=1).then_inc(consts_pool, 1)
            pool.wait_ge(weights_in, 8 * 16)
            fast_pass(pool, pool_graph)
            general_pass(pool, gen_pool)

        @block.tensor
        def _(pe):
            pe.wait_ge(consts_pool, 3)
            pe.wait_ge(consts_dve, 2)
            pe.wait_ge(weights_in, 8 * 16)
            fast_pass(pe, pe_graph)
            pe.wait_ge(over_red, 1)
            pe.transpose(end_ps[0:1, 0, 0, :], over1[:, :], ident32[:, :]).then_inc(over_t, 1)
            general_pass(pe, gen_pe)

        @block.scalar
        def _(act):
            act.wait_ge(consts_pool, 2)
            fast_pass(act, act_graph)
            general_pass(act, gen_act)

        @block.vector
        def _(dve):
            dve.wait_ge(weights_in, 8 * 16)
            dve.tensor_reduce(w1sum[:, :], w1[:, :, :], AX.X, ALU.add)
            dve.tensor_scalar(g1o[:, :], g1b[:, :], math.sqrt(O), None, ALU.mult)
            dve.tensor_reduce(b1sum[:, :], b1r[:, :], AX.X, ALU.add).then_inc(consts_dve, 1)
            dve.wait_ge(consts_dve, 1)
            dve.scalar_tensor_tensor(w1c[:, :, :], w1sum[:, :].unsqueeze(2).to_broadcast([P, 2, O]), -1.0 / O, w1[:, :, :], ALU.mult, ALU.add)
            dve.memset(b1c[:, :, 0:O], 0.0)
            for h in range(NH):
                last = dve.scalar_tensor_tensor(b1c[:, h, O:2 * O], b1sum[:, :].to_broadcast([1, O]), -1.0 / O, b1r[:, :], ALU.mult, ALU.add)
            last.then_inc(consts_dve, 1)
            dve.wait_ge(consts_pool, 2)
            for q in range(RICH_SLOTS):
                for r in range(RANKS):
                    dve.memset(own_rank[r * RICH:(r + 1) * RICH, q:q + 1], float(BASE + q * RANKS + r - N))
            dve.tensor_copy(node_no[:, :], node_i[:, :, :].rearrange("p r m -> p (r m)"))
            dve.tensor_copy(rank_no[:, :, :], rank_i[:, :, :, :].rearrange("p q r m -> p q (r m)")).then_inc(consts_dve, 1)
            dve.wait_ge(consts_dve, 3)
            fast_pass(dve, dve_graph)
            dve.wait_ge(over_done, B)
            dve.tensor_scalar(over_by[:, 0, :], over[:, 0, :], float(CAP), None, ALU.subtract)
            dve.tensor_scalar(over_by[:, 1, :], over[:, 1, :], float(RICH), None, ALU.subtract).then_inc(over_less, 1)
            dve.wait_ge(over_less, 1)
            dve.tensor_reduce(over1[:, :], over_by[:, :, :].rearrange("p a h -> p (a h)"), AX.X, ALU.max).then_inc(over_red, 1)
            dve.wait_ge(over_t, 1)
            dve.tensor_reduce(over2[:, :], end_ps[0:1, 0, 0, :], AX.X, ALU.max).then_inc(over_max, 1)
            dve.wait_ge(over_max, 1)
            dve.tensor_scalar(flag[:, :], over2[:, :], 0.0, None, ALU.is_gt).then_inc(flag_done, 1)
            general_pass(dve, gen_dve)


_INS = ["x", "adj", "L0_gnn_W1", "L0_gnn_b1", "L0_gnn_g1", "L0_gnn_be1", "L0_gnn_W2", "L0_gnn_b2", "L0_gnn_g2", "L0_gnn_be2"]


def kernel(**inputs):
    import numpy as _np
    import concourse.bacc as _bacc
    from concourse import mybir as _mybir
    from concourse.bass_utils import run_bass_kernel_spmd as _run

    nc = _bacc.Bacc("TRN2", target_bir_lowering=False, num_devices=1)
    arrays, aps = {}, {}
    laid_out = {name: _np.ascontiguousarray(inputs[name]) for name in _INS}
    laid_out["xt"] = _np.ascontiguousarray(_np.transpose(laid_out["x"], (0, 2, 1)))
    for name, a in laid_out.items():
        arrays[f"in_{name}"] = a
        aps[name] = nc.dram_tensor(f"in_{name}", a.shape, _mybir.dt.from_np(a.dtype), kind="ExternalInput").ap()
    out = nc.dram_tensor("out_0", (B, N, O), _mybir.dt.float32, kind="ExternalOutput").ap()
    gnn_kernel(nc, aps["x"], aps["xt"], aps["adj"], *(aps[n] for n in _INS[2:]), out)
    r = _run(nc, [arrays], core_ids=[0])
    return r.results[0]["out_0"]
```

```python
import math
from collections import namedtuple
from contextlib import ExitStack

import concourse.bass as bass
from concourse import mybir

B, N, D, O = 32, 256, 128, 128
P = 128
NH = N // P
LN_EPS = 1e-5

BASE = 6
RICH_SLOTS = 3
RICH = 96
RICHEST_PARTS = 2
RICHEST = (P - RICH) // RICHEST_PARTS
RICHER = BASE + RICH_SLOTS
CAP = RICHER + RICHEST_PARTS * RICH_SLOTS
FAST_STEPS = [(0, (0, 1, 2)), (0, (3, 4, 5)), (1, (0, 1, 2)), (1, (3, 4, 5)), (NH, (0, 1, 2))]
NBUF = len(FAST_STEPS)
NBANK = 4
BANKS = (0, 1, 2, 3, 0, 1, 2, 3, 1, 2)
GEN_SLOTS = 12
GEN_STEPS = [(0, 1, 2, 3), (4, 5, 6, 7), (8, 9, 10, 11)]
GEN_ROUNDS = -(-N // GEN_SLOTS)
EXTRACTED = 16

Graph = namedtuple("Graph", "b n par m back r")
Step = namedtuple("Step", "s a bank bank_back buf back h slots")


def gnn_kernel(nc, x, xt, adj, W1, b1, g1, be1, W2, b2, g2, be2, out):
    fp32, bf16, i32, u16 = mybir.dt.float32, mybir.dt.bfloat16, mybir.dt.int32, mybir.dt.uint16
    ALU, ACT, AX = mybir.AluOpType, mybir.ActivationFunctionType, mybir.AxisListType
    S = len(FAST_STEPS)
    KTOT = sum(len(slots) for _, slots in FAST_STEPS)

    ctx = ExitStack()
    with ctx:
        def sb(name, shape, dt=fp32):
            return ctx.enter_context(nc.sbuf_tensor(name, shape, dt))

        def ps(name, shape, dt=fp32):
            return ctx.enter_context(nc.psum_tensor(name, shape, dt))

        def sem(name):
            return ctx.enter_context(nc.semaphore(name))

        ident = sb("ident", [P, P], bf16)
        minus_ident = sb("minus_ident", [P, P], bf16)
        ident32 = sb("ident32", [P, P])
        upto = sb("upto", [P, P], bf16)
        upto_edge = sb("upto_edge", [P, P], bf16)
        ones = sb("ones", [P, P], bf16)
        ones_row = sb("ones_row", [1, P])
        order = sb("order", [P, NH, N])
        order_i = sb("order_i", [P, NH, N], i32)
        minus_half = sb("minus_half", [P, 4])
        eps = sb("eps", [P, 4])
        eps_o = sb("eps_o", [P, 4])
        slot_no = sb("slot_no", [P, GEN_SLOTS])
        slot_i = sb("slot_i", [P, GEN_SLOTS], i32)
        node_no = sb("node_no", [P, P], bf16)
        node_i = sb("node_i", [P, P], i32)
        rank_no = sb("rank_no", [P, RICH_SLOTS, P], bf16)
        rank_i = sb("rank_i", [P, RICH_SLOTS, P], i32)
        own_rank = sb("own_rank", [P, RICH_SLOTS])
        w1 = sb("w1", [P, 2, O])
        w1sum = sb("w1sum", [P, 2])
        w1c = sb("w1c", [P, 2, O])
        w2 = sb("w2", [P, 2, O])
        w2sum = sb("w2sum", [P, 2])
        w2c = sb("w2c", [P, 2, O])
        b1r = sb("b1r", [1, O])
        b1sum = sb("b1sum", [1, 1])
        b1c = sb("b1c", [1, NH, 2 * O])
        b2r = sb("b2r", [1, O])
        b2sum = sb("b2sum", [1, 1])
        b2c = sb("b2c", [1, O])
        g1b = sb("g1b", [P, O])
        g1o = sb("g1o", [P, O])
        be1b = sb("be1b", [P, O])
        g2b = sb("g2b", [P, O])
        g2o = sb("g2o", [P, O])
        be2b = sb("be2b", [P, O])

        adj_sb = sb("adj_sb", [P, 2, NH, N])
        xt_sb = sb("xt_sb", [P, 2, N])
        xt_late = sb("xt_late", [P, 2, N])
        x_sb = sb("x_sb", [P, 2, NH, D])
        mask = sb("mask", [P, 2, NH, N], bf16)
        mask_t = sb("mask_t", [P, NH, N], bf16)
        rank_t = sb("rank_t", [P, 2, NH, N], bf16)
        tab = sb("tab", [P, 2, 3, NH, 2 * O], bf16)
        adj_n = sb("adj_n", [P, NH, N])
        halves = sb("halves", [P, 2, NH, N])
        place = sb("place", [P, NH, N])
        key = sb("key", [P, 2, NH, N])
        key2 = sb("key2", [P, NH, 2, N])
        top = sb("top", [P, 2, NH, 2, EXTRACTED])
        top_i = sb("top_i", [P, NH, 2, EXTRACTED], i32)
        wgt = sb("wgt", [P, 2, NH, EXTRACTED])
        agg = sb("agg", [P, 2, NH, O])
        agg_t = sb("agg_t", [P, NH, P])
        over = sb("over", [P, 3 * NH])
        least = sb("least", [P, 2])
        limit = sb("limit", [P, 3 * NH])

        rich = sb("rich", [P, NH, 2], bf16)
        rich_at = sb("rich_at", [P, NH, 2])
        sel = sb("sel", [P, 2, NH, P], bf16)
        sel32 = sb("sel32", [P, NH, P])
        sel_t = sb("sel_t", [P, 2, NH, P])
        mask_r = sb("mask_r", [P, NH, P], bf16)
        rank_r = sb("rank_r", [P, NH, P], bf16)
        adj_r = sb("adj_r", [P, N])
        chosen = sb("chosen", [P, 2, RICH_SLOTS, N])
        wgt_r = sb("wgt_r", [P, 2, RICH_SLOTS])
        agg_r = sb("agg_r", [P, O])

        onehot = sb("onehot", [P, NBUF, 4, NH, P], bf16)
        squares = sb("squares", [P, NBUF, 4, O], bf16)
        ssq = sb("ssq", [P, NBUF, 4])
        var1 = sb("var1", [P, NBUF, 4])
        rstd = sb("rstd", [P, NBUF, 4])
        msg = sb("msg", [P, NBUF, 4, O])

        squares2 = sb("squares2", [P, NH, O], bf16)
        ssq2 = sb("ssq2", [P, NH])
        veps = sb("veps", [P, NH])
        rstd2 = sb("rstd2", [P, NH])
        upd = sb("upd", [P, NH, O])
        stats3 = sb("stats3", [P, NH, 6])
        moments3 = sb("moments3", [P, NH, 2])
        veps3 = sb("veps3", [P, NH])
        rstd3 = sb("rstd3", [P, NH])
        y = sb("y", [P, 2, NH, O])
        carrier = sb("carrier", [P, 6])
        over_by = sb("over_by", [P, 3 * NH])
        over1 = sb("over1", [P, 1])
        over2 = sb("over2", [1, 1])
        flag = sb("flag", [1, 1], i32)

        pre = [ps(f"pre{i}", [P, 4, O]) for i in range(NBANK)]
        tab_ps = ps("tab_ps", [P, NH, 2 * O])
        turn_ps = ps("turn_ps", [P, 2 * N])
        rank_ps = turn_ps[:, :].rearrange("p (h j) -> p h j", h=NH)
        end_ps = turn_ps[:, :].rearrange("p (a h j) -> p a h j", a=2, h=NH)
        rich_ps = ps("rich_ps", [P, 2, N])
        small_ps = ps("small_ps", [P, 2 * N])
        mask_ps = small_ps[:, 0:N].bitcast(bf16).rearrange("p (h j) -> p h j", h=NH)
        sel_ps = small_ps[:, N:N + P].bitcast(bf16).rearrange("p (h j) -> p h j", h=NH)
        counts_ps = small_ps[:, N + P:N + P + 3 * NH]
        upto_ps = counts_ps[:, NH:3 * NH].rearrange("p (h a) -> p h a", h=NH)
        own_ps = small_ps[:, N + P + 3 * NH:N + P + 3 * NH + RICH_SLOTS]

        weights_in = sem("weights_in")
        consts_pool = sem("consts_pool")
        consts_dve = sem("consts_dve")
        own_psd = sem("own_psd")
        adj_in = [sem("adj_in0"), sem("adj_in1")]
        xt_in = [sem("xt_in0"), sem("xt_in1")]
        x_in = [sem("x_in0"), sem("x_in1")]
        late_in = [sem("late_in0"), sem("late_in1")]
        mask_done = sem("mask_done")
        maskt_ps = sem("maskt_ps")
        maskt_sb = sem("maskt_sb")
        rank_psd = sem("rank_psd")
        rank_done = sem("rank_done")
        tab_psd = sem("tab_psd")
        hi_done = sem("hi_done")
        less_hi = sem("less_hi")
        mid_done = sem("mid_done")
        less_mid = sem("less_mid")
        tab_done = sem("tab_done")
        adjn_done = sem("adjn_done")
        place_done = sem("place_done")
        halves_done = sem("halves_done")
        keys_done = sem("keys_done")
        top8 = sem("top8")
        cut = sem("cut")
        top_done = sem("top_done")
        topi_done = sem("topi_done")
        wgt_done = sem("wgt_done")
        over_done = sem("over_done")
        deg_psd = sem("deg_psd")
        rich_done = sem("rich_done")
        richat_psd = sem("richat_psd")
        richat_done = sem("richat_done")
        sel_done = sem("sel_done")
        sel32_done = sem("sel32_done")
        selt_psd = sem("selt_psd")
        maskr_psd = sem("maskr_psd")
        adjr_psd = sem("adjr_psd")
        selt_done = sem("selt_done")
        maskr_done = sem("maskr_done")
        adjr_done = sem("adjr_done")
        rankr_psd = sem("rankr_psd")
        rankr_done = sem("rankr_done")
        wgtr_done = sem("wgtr_done")
        onehot_done = sem("onehot_done")
        pre_done = sem("pre_done")
        ssq_done = sem("ssq_done")
        var_done = sem("var_done")
        rstd_done = sem("rstd_done")
        norm_done = sem("norm_done")
        shift_done = sem("shift_done")
        gelu_done = sem("gelu_done")
        acc_done = sem("acc_done")
        aggt_ps = sem("aggt_ps")
        aggt_sb = sem("aggt_sb")
        upd_ps = sem("upd_ps")
        ssq2_done = sem("ssq2_done")
        veps_done = sem("veps_done")
        rstd2_done = sem("rstd2_done")
        updn_done = sem("updn_done")
        y_steps = sem("y_steps")
        st3_done = sem("st3_done")
        mom3_done = sem("mom3_done")
        veps3_done = sem("veps3_done")
        rstd3_done = sem("rstd3_done")
        y_done = sem("y_done")
        out_written = [sem("out_written0"), sem("out_written1")]
        over_less = sem("over_less")
        over_red = sem("over_red")
        over_t = sem("over_t")
        over_max = sem("over_max")
        flag_done = sem("flag_done")
        gen_kept = sem("gen_kept")
        gen_slot = sem("gen_slot")

        def wait(eng, s, value):
            if not isinstance(value, int) or value > 0:
                eng.wait_ge(s, value)


        def load_adj(G, fast=True):
            wait(nc.sync, mask_done, G.n - G.back)
            wait(nc.sync, adjn_done, G.n - G.back)
            if fast:
                wait(nc.sync, adjr_psd, G.n - G.back)
            nc.sync.dma_start(adj_sb[:, G.par], adj[G.b].rearrange("(h p) j -> p h j", p=P)).then_inc(adj_in[G.par], 16)

        def load_xt(G):
            wait(nc.sync, tab_psd, G.n - G.back)
            nc.sync.dma_start(xt_sb[:, G.par], xt[G.b]).then_inc(xt_in[G.par], 16)

        def load_xt_late(G):
            wait(nc.sync, upd_ps, G.n - G.back)
            nc.sync.dma_start(xt_late[:, G.par], xt[G.b]).then_inc(late_in[G.par], 16)

        def load_x(G):
            wait(nc.sync, y_steps, 3 * (G.n - G.back))
            nc.sync.dma_start(x_sb[:, G.par], x[G.b].rearrange("(h p) d -> p h d", p=P)).then_inc(x_in[G.par], 16)

        def store_y(G):
            nc.sync.wait_ge(y_done, G.n)
            nc.sync.dma_start(out[G.b].rearrange("(h p) o -> p h o", p=P), y[:, G.par]).then_inc(out_written[G.par], 16)

        def transpose_mask(G):
            nc.tensor.wait_ge(mask_done, G.n)
            wait(nc.tensor, maskt_sb, G.n - 1)
            wait(nc.tensor, over_done, G.r)
            for h in range(NH):
                for jb in range(NH):
                    last = nc.tensor.transpose(mask_ps[:, jb, h * P:(h + 1) * P], mask[:, G.par, h, jb * P:(jb + 1) * P], ident[:, :])
            last.then_inc(maskt_ps, 1)

        def rank_product(G, updates):
            nc.tensor.wait_ge(maskt_sb, G.n)
            wait(nc.tensor, rank_done, G.n - 1)
            wait(nc.tensor, updn_done, updates)
            nc.tensor.matmul(rank_ps[:, 0, :], upto_edge[:, :], mask_t[:, 0, :], start=True, stop=True)
            nc.tensor.matmul(rank_ps[:, 1, :], ones[:, :], mask_t[:, 0, :], start=True, stop=False)
            nc.tensor.matmul(rank_ps[:, 1, :], upto_edge[:, :], mask_t[:, 1, :], start=False, stop=True).then_inc(rank_psd, 1)

        def table_product(G):
            nc.tensor.wait_ge(xt_in[G.par], 16 * G.m)
            wait(nc.tensor, tab_done, G.n - 1)
            nc.tensor.matmul(tab_ps[:, :, :].rearrange("p h o -> p (h o)"), ones_row[:, :],
                             b1c[:, :, :].rearrange("p h o -> p (h o)"), start=True, stop=False, skip_group_check=True)
            for h in range(NH):
                last = nc.tensor.matmul(tab_ps[:, h, :], xt_sb[:, G.par, h * P:(h + 1) * P],
                                        w1c[:, :, :].rearrange("p a o -> p (a o)"), start=False, stop=True, skip_group_check=True)
            last.then_inc(tab_psd, 1)

        def table_less(G, part, taken, done):
            nc.tensor.wait_ge(taken, G.n)
            nc.tensor.matmul(tab_ps[:, :, :].rearrange("p h o -> p (h o)"), minus_ident[:, :],
                             tab[:, G.par, part].rearrange("p h o -> p (h o)"), start=False, stop=True, skip_group_check=True).then_inc(done, 1)

        def degrees(G):
            nc.tensor.wait_ge(maskt_sb, G.n)
            wait(nc.tensor, selt_done, G.r)
            for h in range(NH):
                for jb in range(NH):
                    last = nc.tensor.matmul(counts_ps[:, h:h + 1], mask_t[:, jb, h * P:(h + 1) * P], ones[:, 0:1],
                                            start=(jb == 0), stop=(jb == NH - 1))
            last.then_inc(deg_psd, 1)

        def count_rich(G):
            nc.tensor.wait_ge(rich_done, G.n)
            nc.tensor.matmul(upto_ps[:, 0, :], upto[:, :], rich[:, 0, :], start=True, stop=True)
            nc.tensor.matmul(upto_ps[:, 1, :], ones[:, :], rich[:, 0, :], start=True, stop=False)
            nc.tensor.matmul(upto_ps[:, 1, :], upto[:, :], rich[:, 1, :], start=False, stop=True).then_inc(richat_psd, 1)

        def transpose_sel(G):
            pe = nc.tensor
            pe.wait_ge(sel_done, G.n)
            pe.wait_ge(over_done, G.n)
            for h in range(NH):
                last = pe.transpose(sel_ps[:, h, :], sel[:, G.par, h, :], ident[:, :])
            last.then_inc(selt_psd, 1)

        def rich_products(G):
            pe = nc.tensor
            wait(pe, rankr_done, G.n - 1)
            wait(pe, wgtr_done, G.n - 1)
            for jb in range(NH):
                for h in range(NH):
                    last = pe.matmul(rich_ps[:, 0, jb * P:(jb + 1) * P], mask[:, G.par, h, jb * P:(jb + 1) * P], sel[:, G.par, h, :],
                                     start=(h == 0), stop=(h == NH - 1))
            last.then_inc(maskr_psd, 1)
            pe.wait_ge(sel32_done, G.n)
            for h in range(NH):
                last = pe.matmul(rich_ps[:, 1, :], sel32[:, h, :], adj_sb[:, G.par, h, :], start=(h == 0), stop=(h == NH - 1))
            last.then_inc(adjr_psd, 1)

        def rich_rank_products(G):
            pe = nc.tensor
            pe.wait_ge(maskr_done, G.n)
            pe.wait_ge(adjr_done, G.n)
            pe.matmul(rich_ps[:, 0, 0:P], upto_edge[:, :], mask_r[:, 0, :], start=True, stop=True)
            pe.matmul(rich_ps[:, 0, P:N], ones[:, :], mask_r[:, 0, :], start=True, stop=False)
            pe.matmul(rich_ps[:, 0, P:N], upto_edge[:, :], mask_r[:, 1, :], start=False, stop=True)
            pe.matmul(rich_ps[:, 1, 0:P], mask_r[:, 0, :], upto_edge[:, :], start=True, stop=True)
            pe.matmul(rich_ps[:, 1, P:N], mask_r[:, 0, :], ones[:, :], start=True, stop=False)
            pe.matmul(rich_ps[:, 1, P:N], mask_r[:, 1, :], upto_edge[:, :], start=False, stop=True).then_inc(rankr_psd, 1)

        def gather(G, T):
            nc.tensor.wait_ge(onehot_done, T.s + 1)
            nc.tensor.wait_ge(tab_done, G.n)
            wait(nc.tensor, norm_done, T.s - T.bank_back + 1)
            kn = len(T.slots)
            own = [(sel[:, G.par, h, :], h) for h in range(NH)] if T.h == NH else [(ident[:, :], T.h)]
            for a, (pick, h) in enumerate(own):
                for part in range(3):
                    nc.tensor.matmul(pre[T.bank][:, 0:kn, :], pick,
                                     tab[:, G.par, part, h, O:2 * O].unsqueeze(1).to_broadcast([P, kn, O]),
                                     start=(a == 0 and part == 0), stop=False, skip_group_check=True)
            for q in range(kn):
                for jb in range(NH):
                    for part in range(3):
                        last = nc.tensor.matmul(pre[T.bank][:, q, :], onehot[:, T.buf, q, jb, :],
                                                tab[:, G.par, part, jb, 0:O], start=False,
                                                stop=(jb == NH - 1 and part == 2), skip_group_check=True)
            last.then_inc(pre_done, 1)

        def transpose_agg(G, a_end, ranks, fast=True):
            nc.tensor.wait_ge(acc_done, a_end)
            wait(nc.tensor, updn_done, G.n - 1)
            nc.tensor.wait_ge(rank_done, ranks)
            if fast:
                nc.tensor.wait_ge(selt_done, G.n)
                nc.tensor.matmul(end_ps[:, 0, :, :], agg_r[:, :], sel_t[:, G.par], start=True, stop=False, skip_group_check=True)
            for h in range(NH):
                last = nc.tensor.matmul(end_ps[:, 0, h, :], agg[:, G.par, h, :], ident32[:, :], start=not fast, stop=True, skip_group_check=True)
            last.then_inc(aggt_ps, 1)

        def update_product(G):
            nc.tensor.wait_ge(aggt_sb, G.n)
            nc.tensor.wait_ge(late_in[G.par], 16 * G.m)
            for h in range(NH):
                nc.tensor.matmul(end_ps[:, 1, h, :], xt_late[:, G.par, h * P:(h + 1) * P], w2c[:, 0, :], start=True, stop=False)
                nc.tensor.matmul(end_ps[:, 1, h, :], agg_t[:, h, :], w2c[:, 1, :], start=False, stop=False)
                last = nc.tensor.matmul(end_ps[:, 1, h, :], ones_row[:, :], b2c[:, :], start=False, stop=True)
            last.then_inc(upd_ps, 1)

        def copy_mask(G, mask_free):
            nc.scalar.wait_ge(maskt_ps, G.n)
            wait(nc.scalar, rank_psd, G.n - 1)
            wait(nc.scalar, deg_psd, mask_free)
            nc.scalar.copy(mask_t[:, :, :], mask_ps[:, :, :]).then_inc(maskt_sb, 1)

        def copy_rank(G, s_free):
            nc.scalar.wait_ge(rank_psd, G.n)
            wait(nc.scalar, onehot_done, s_free)
            nc.scalar.copy(rank_t[:, G.par], rank_ps[:, :, :]).then_inc(rank_done, 1)

        def copy_rich_rank(G):
            nc.scalar.wait_ge(rankr_psd, G.n)
            wait(nc.scalar, onehot_done, S * (G.n - 1))
            nc.scalar.copy(rank_r[:, :, :], rich_ps[:, 0, :].rearrange("p (h j) -> p h j", h=NH)).then_inc(rankr_done, 1)

        def plus_zero(G):
            nc.scalar.wait_ge(adj_in[G.par], 16 * G.m)
            wait(nc.scalar, halves_done, 2 * (G.n - 1))
            nc.scalar.activation(adj_n[:, :, :], adj_sb[:, G.par], ACT.Identity).then_inc(adjn_done, 1)

        def split_bits(G, half):
            nc.scalar.wait_ge(adjn_done, G.n)
            wait(nc.scalar, keys_done, 2 * G.n - 3 + half)
            bits = adj_n[:, :, :].bitcast(u16).rearrange("p h (j t) -> p t h j", t=2)
            nc.scalar.copy(halves[:, half], bits[:, half]).then_inc(halves_done, 1)

        def copy_sel(G):
            nc.scalar.wait_ge(sel_done, G.n)
            wait(nc.scalar, adjr_psd, G.n - 1)
            nc.scalar.copy(sel32[:, :, :], sel[:, G.par]).then_inc(sel32_done, 1)

        def copy_rich(G):
            act = nc.scalar
            act.wait_ge(adjr_psd, G.n)
            wait(act, rankr_psd, G.n - 1)
            act.copy(mask_r[:, :, :], rich_ps[:, 0, :].rearrange("p (h j) -> p h j", h=NH)).then_inc(maskr_done, 1)
            wait(act, wgtr_done, G.n - 1)
            act.copy(adj_r[:, :], rich_ps[:, 1, :]).then_inc(adjr_done, 1)

        def copy_sel_t(G):
            act = nc.scalar
            act.wait_ge(selt_psd, G.n)
            wait(act, aggt_ps, G.n - 2)
            act.copy(sel_t[:, G.par], sel_ps[:, :, :]).then_inc(selt_done, 1)

        def table_hi(G, s_free):
            nc.scalar.wait_ge(tab_psd, G.n)
            wait(nc.scalar, pre_done, s_free)
            nc.scalar.copy(tab[:, G.par, 0], tab_ps[:, :, :]).then_inc(hi_done, 1)

        def table_rest(G, part, left, done):
            nc.scalar.wait_ge(left, G.n)
            nc.scalar.copy(tab[:, G.par, part], tab_ps[:, :, :]).then_inc(done, 1)

        def square(T):
            nc.scalar.wait_ge(pre_done, T.s + 1)
            wait(nc.scalar, rstd_done, T.s - T.back + 1)
            for q in range(len(T.slots)):
                last = nc.scalar.activation(squares[:, T.buf, q, :], pre[T.bank][:, q, :], ACT.Square, accum_out=ssq[:, T.buf, q:q + 1])
            last.then_inc(ssq_done, 1)
            nc.scalar.wait_ge(ssq_done, T.s + 1)
            kn = len(T.slots)
            nc.scalar.activation(var1[:, T.buf, 0:kn], ssq[:, T.buf, 0:kn], ACT.Identity, bias=eps_o[:, 0:1]).then_inc(var_done, 1)

        def gelu(T):
            nc.scalar.wait_ge(shift_done, T.s + 1)
            kn = len(T.slots)
            nc.scalar.activation(msg[:, T.buf, 0:kn, :], msg[:, T.buf, 0:kn, :], ACT.Gelu).then_inc(gelu_done, 1)

        def make_weights(G, t, wgt_free, width):
            act = nc.scalar
            act.wait_ge(top_done, t)
            wait(act, wgt_done, t - 1)
            wait(act, acc_done, wgt_free)
            act.copy(top_i[:, :, :, 0:width], top[:, G.par, :, :, 0:width]).then_inc(topi_done, 1)
            act.wait_ge(topi_done, t)
            low = top_i[:, :, :, 0:width].bitcast(u16).rearrange("p h t (k u) -> p u t h k", u=2)
            to = wgt[:, G.par, :, 0:width].bitcast(u16).rearrange("p h (k u) -> p u h k", u=2)
            act.copy(to[:, 1], low[:, 0, 0])
            act.copy(to[:, 0], low[:, 0, 1]).then_inc(wgt_done, 1)

        def copy_agg_t(G):
            nc.scalar.wait_ge(aggt_ps, G.n)
            wait(nc.scalar, upd_ps, G.n - 1)
            nc.scalar.copy(agg_t[:, :, :], end_ps[:, 0]).then_inc(aggt_sb, 1)

        def update_square(G):
            act = nc.scalar
            act.wait_ge(upd_ps, G.n)
            for h in range(NH):
                last = act.activation(squares2[:, h, :], end_ps[:, 1, h, :], ACT.Square, accum_out=ssq2[:, h:h + 1])
            last.then_inc(ssq2_done, 1)
            act.wait_ge(ssq2_done, G.n)
            wait(act, rstd2_done, G.n - 1)
            act.activation(veps[:, :], ssq2[:, :], ACT.Identity, bias=eps_o[:, 0:1]).then_inc(veps_done, 1)

        def out_var(G):
            nc.scalar.wait_ge(mom3_done, G.n)
            wait(nc.scalar, rstd3_done, G.n - 1)
            nc.scalar.activation(veps3[:, :], moments3[:, :, 1], ACT.Identity, bias=eps[:, 0:1]).then_inc(veps3_done, 1)

        def update_norm(G):
            act = nc.scalar
            act.wait_ge(rstd2_done, G.n)
            wait(act, y_steps, 3 * (G.n - 1))
            for h in range(NH):
                last = act.activation(upd[:, h, :], end_ps[:, 1, h, :], ACT.Identity, scale=rstd2[:, h:h + 1])
            last.then_inc(updn_done, 1)

        def make_key(G, half, top_free):
            pool = nc.gpsimd
            pool.wait_ge(place_done, G.n)
            wait(pool, top_done, top_free)
            pool.wait_ge(halves_done, 2 * (G.n - 1) + 1 + half)
            pool.tensor_tensor(key[:, 1 - half], place[:, :, :], halves[:, half], ALU.add).then_inc(keys_done, 1)

        def rsqrt(T):
            pool = nc.gpsimd
            kn = len(T.slots)
            pool.wait_ge(var_done, T.s + 1)
            wait(pool, norm_done, T.s - T.back + 1)
            pool.tensor_tensor(rstd[:, T.buf, 0:kn], var1[:, T.buf, 0:kn], minus_half[:, 0:kn], ALU.pow).then_inc(rstd_done, 1)

        def shift(T):
            pool = nc.gpsimd
            kn = len(T.slots)
            pool.wait_ge(norm_done, T.s + 1)
            m = msg[:, T.buf, 0:kn, :]
            pool.tensor_tensor(m, m, be1b[:, :].unsqueeze(1).to_broadcast([P, kn, O]), ALU.add).then_inc(shift_done, 1)

        def rstd_update(G):
            pool = nc.gpsimd
            pool.wait_ge(veps_done, G.n)
            wait(pool, updn_done, G.n - 1)
            pool.tensor_tensor(rstd2[:, :], veps[:, :], minus_half[:, 0:NH], ALU.pow).then_inc(rstd2_done, 1)

        def residual(G):
            pool = nc.gpsimd
            def wide(v):
                return v[:, :].unsqueeze(1).to_broadcast([P, NH, O])
            pool.wait_ge(updn_done, G.n)
            wait(pool, out_written[G.par], 16 * (G.m - 1))
            pool.tensor_tensor(y[:, G.par], upd[:, :, :], wide(g2o), ALU.mult).then_inc(y_steps, 1)
            pool.wait_ge(y_steps, 3 * G.n - 2)
            pool.tensor_tensor(y[:, G.par], y[:, G.par], wide(be2b), ALU.add).then_inc(y_steps, 1)
            pool.wait_ge(y_steps, 3 * G.n - 1)
            pool.wait_ge(x_in[G.par], 16 * G.m)
            pool.tensor_tensor(y[:, G.par], y[:, G.par], x_sb[:, G.par], ALU.add).then_inc(y_steps, 1)

        def rstd_out(G):
            pool = nc.gpsimd
            pool.wait_ge(veps3_done, G.n)
            wait(pool, y_done, G.n - 1)
            pool.tensor_tensor(rstd3[:, :], veps3[:, :], minus_half[:, 0:NH], ALU.pow).then_inc(rstd3_done, 1)

        def make_mask(G, rich_free):
            dve = nc.vector
            dve.wait_ge(adj_in[G.par], 16 * G.m)
            wait(dve, maskt_ps, G.n - G.back)
            wait(dve, place_done, G.n - G.back)
            wait(dve, maskr_psd, rich_free)
            dve.tensor_scalar(mask[:, G.par], adj_sb[:, G.par], 0.0, None, ALU.not_equal).then_inc(mask_done, 1)

        def make_places(G):
            dve = nc.vector
            dve.wait_ge(mask_done, G.n)
            wait(dve, keys_done, 2 * (G.n - 1))
            dve.tensor_tensor(place[:, :, :], mask[:, G.par], order[:, :, :], ALU.mult).then_inc(place_done, 1)

        def extract(G, t, tiles):
            dve = nc.vector
            dve.wait_ge(keys_done, 2 * G.n)
            wait(dve, topi_done, t - 1)
            column = 5 * tiles[0]
            dve.memset(carrier[:, column:column + 1], 0.0)
            for h in tiles:
                for u in range(2):
                    last = dve.max(top[:, G.par, h, u, 0:8], key[:, u, h, :])
            return last

        def extract_first(G, h):
            last = extract(G, G.n, (h,))
            if h == NH - 1:
                last.then_inc(top_done, 1)

        def extract_more(G, t):
            dve = nc.vector
            extract(G, t, range(NH)).then_inc(top8, 1)
            dve.wait_ge(top8, t - B)
            for h in range(NH):
                wait(dve, top_done, t - 1)
                for u in range(2):
                    last = dve.scalar_tensor_tensor(key2[:, h, u, :], key[:, u, h, :], top[:, G.par, h, u, 7:8], key[:, u, h, :],
                                                    ALU.is_lt, ALU.mult)
                last.then_inc(cut, 1)
                dve.wait_ge(cut, NH * (t - B - 1) + h + 1)
                dve.memset(carrier[:, 1 + h:2 + h], 0.0)
                for u in range(2):
                    last = dve.max(top[:, G.par, h, u, 8:16], key2[:, h, u, :])
            last.then_inc(top_done, 1)

        def find_rich(G):
            dve = nc.vector
            dve.wait_ge(deg_psd, G.n)
            wait(dve, richat_psd, G.n - 1)
            wait(dve, richat_done, G.n - 1)
            dve.tensor_tensor(rich[:, :, :], counts_ps[:, 0:NH].unsqueeze(2).to_broadcast([P, NH, 2]),
                              least[:, :].unsqueeze(1).to_broadcast([P, NH, 2]), ALU.is_gt).then_inc(rich_done, 1)

        def number_rich(G):
            dve = nc.vector
            dve.wait_ge(richat_psd, G.n)
            wait(dve, sel_done, G.n - 1)
            dve.tensor_tensor(rich_at[:, :, :], upto_ps, rich[:, :, :], ALU.mult).then_inc(richat_done, 1)
            wait(dve, over_done, G.n - 1)
            dve.tensor_tensor(over[:, :], over[:, :], counts_ps, ALU.max).then_inc(over_done, 1)

        def select_rich(G, s_free):
            dve = nc.vector
            dve.wait_ge(richat_done, G.n)
            wait(dve, sel32_done, G.n - 2)
            wait(dve, pre_done, s_free)
            for a, parts in enumerate((slice(0, RICH), slice(RICH, P))):
                shape = [P, NH, parts.stop - parts.start]
                last = dve.tensor_tensor(sel[:, G.par, :, parts], node_no[:, parts].unsqueeze(1).to_broadcast(shape),
                                         rich_at[:, :, a:a + 1].to_broadcast(shape), ALU.is_equal)
            last.then_inc(sel_done, 1)

        def rich_weights(G, a_free):
            dve = nc.vector
            dve.wait_ge(adjr_done, G.n)
            dve.wait_ge(rankr_done, G.n)
            wait(dve, acc_done, a_free)
            for q in range(RICH_SLOTS):
                last = dve.scalar_tensor_tensor(chosen[:, G.par, q, :], rich_ps[:, 1, :], own_rank[:, q:q + 1], adj_r[:, :],
                                                ALU.is_equal, ALU.mult, accum_out=wgt_r[:, G.par, q:q + 1])
            last.then_inc(wgtr_done, 1)

        def make_onehot(G, T, slot_ap=False):
            dve = nc.vector
            dve.wait_ge(rank_done, G.n)
            wait(dve, pre_done, T.s - T.back + 1)
            if T.h == NH:
                dve.wait_ge(rankr_done, G.n)
                kn = len(T.slots)
                dve.tensor_tensor(onehot[:, T.buf, 0:kn], rank_r[:, :, :].unsqueeze(1).to_broadcast([P, kn, NH, P]),
                                  rank_no[:, :, :].unsqueeze(2).to_broadcast([P, kn, NH, P]), ALU.is_equal).then_inc(onehot_done, 1)
                return
            for q, k in enumerate(T.slots):
                value = slot_no[:, k:k + 1] if slot_ap else float(k - N)
                last = dve.tensor_scalar(onehot[:, T.buf, q], rank_t[:, G.par, :, T.h * P:(T.h + 1) * P], value, None, ALU.is_equal)
            last.then_inc(onehot_done, 1)

        def norm_slot(T, q):
            dve = nc.vector
            if q == 0:
                dve.wait_ge(rstd_done, T.s + 1)
            ins = dve.scalar_tensor_tensor(msg[:, T.buf, q, :], pre[T.bank][:, q, :], rstd[:, T.buf, q:q + 1], g1o[:, :], ALU.mult, ALU.mult)
            if q == len(T.slots) - 1:
                ins.then_inc(norm_done, 1)

        def acc_slot(G, T, q, t, agg_free=None):
            dve = nc.vector
            is_rich = T.h == NH
            if q == 0:
                dve.wait_ge(gelu_done, T.s + 1)
                if is_rich:
                    dve.wait_ge(wgtr_done, G.n)
                else:
                    dve.wait_ge(wgt_done, t)
            first = agg_free is not None and T.slots[q] == 0
            if first:
                wait(dve, aggt_ps, agg_free)
            else:
                dve.wait_ge(acc_done, T.a + q)
            k = T.slots[q]
            a = agg_r[:, :] if is_rich else agg[:, G.par, T.h, :]
            w = wgt_r[:, G.par, k:k + 1] if is_rich else wgt[:, G.par, T.h, k:k + 1]
            if first:
                ins = dve.tensor_scalar(a, msg[:, T.buf, q, :], w, None, ALU.mult)
            else:
                ins = dve.scalar_tensor_tensor(a, msg[:, T.buf, q, :], w, a, ALU.mult, ALU.add)
            ins.then_inc(acc_done, 1)

        def out_moments(G):
            dve = nc.vector
            dve.wait_ge(y_steps, 3 * G.n)
            for h in range(NH):
                last = dve.bn_stats(stats3[:, h, :], y[:, G.par, h, :])
            last.then_inc(st3_done, 1)
            dve.wait_ge(st3_done, G.n)
            wait(dve, veps3_done, G.n - 1)
            dve.memset(carrier[:, 4:5], 0.0)
            for h in range(NH):
                last = dve.bn_aggr(moments3[:, h, :], stats3[:, h, :])
            last.then_inc(mom3_done, 1)

        def out_norm(G):
            dve = nc.vector
            dve.wait_ge(rstd3_done, G.n)
            for h in range(NH):
                last = dve.tensor_scalar(y[:, G.par, h, :], y[:, G.par, h, :], moments3[:, h, 0:1], rstd3[:, h:h + 1], ALU.subtract, ALU.mult)
            last.then_inc(y_done, 1)


        def graph(g, c):
            return Graph(2 * g + c, 2 * g + c + 1, c % 2, g + c // 2 + 1, 2, 2 * g + c)

        def step(g, c, i):
            c, i = c + i // S, i % S
            h, slots = FAST_STEPS[i]
            before = sum(len(v) for _, v in FAST_STEPS[:i])
            at = c % 2 * S + i
            bank_back = next(n for n in range(1, 2 * S + 1) if BANKS[(at - n) % (2 * S)] == BANKS[at])
            return graph(g, c), Step((2 * g + c) * S + i, (2 * g + c) * KTOT + before, BANKS[at], bank_back, i, NBUF, h, slots)

        def there(g, c, i=0):
            return not isinstance(g, int) or 0 <= 2 * g + c + i // S < B

        def sp_graph(g, c):
            if there(g, c + 2):
                load_xt(graph(g, c + 2))
            if there(g, c):
                load_xt_late(graph(g, c))
            if there(g, c + 2):
                load_adj(graph(g, c + 2))
            if there(g, c):
                load_x(graph(g, c))
            if there(g, c - 3):
                store_y(graph(g, c - 3))

        def pe_graph(g, c):
            for i in range(S):
                if there(g, c):
                    gather(*step(g, c, i))
                if i == 0 and there(g, c + 1):
                    table_product(graph(g, c + 1))
                if i == 1 and there(g, c + 1):
                    table_less(graph(g, c + 1), 0, hi_done, less_hi)
                if i == 1 and there(g, c):
                    transpose_sel(graph(g, c))
                if i == 1 and there(g, c + 1):
                    transpose_mask(graph(g, c + 1))
                if i == 1 and there(g, c):
                    rich_products(graph(g, c))
                if i == 2 and there(g, c):
                    rich_rank_products(graph(g, c))
                if i == 2 and there(g, c + 1):
                    rank_product(graph(g, c + 1), 2 * g + c - 1)
                if i == 3 and there(g, c + 1):
                    degrees(graph(g, c + 1))
                    table_less(graph(g, c + 1), 1, mid_done, less_mid)
                if i == 3 and there(g, c - 1):
                    transpose_agg(graph(g, c - 1), (2 * g + c) * KTOT, 2 * g + c + 2 if there(g, c + 1) else B)
                if i == 4 and there(g, c + 1):
                    count_rich(graph(g, c + 1))
                if i == 4 and there(g, c - 1):
                    update_product(graph(g, c - 1))

        def act_graph(g, c):
            for i in range(S):
                if there(g, c, i):
                    square(step(g, c, i)[1])
                if there(g, c, i - 2):
                    gelu(step(g, c, i - 2)[1])
                if i == 0 and there(g, c):
                    copy_sel(graph(g, c))
                if i == 0 and there(g, c + 1):
                    table_hi(graph(g, c + 1), S * (2 * g + c))
                    plus_zero(graph(g, c + 1))
                if i == 0 and there(g, c - 3):
                    out_var(graph(g, c - 3))
                if i == 0 and there(g, c - 2):
                    update_norm(graph(g, c - 2))
                if i == 1 and there(g, c + 1):
                    copy_mask(graph(g, c + 1), 2 * g + c + 1)
                if i == 1 and there(g, c):
                    copy_sel_t(graph(g, c))
                    copy_rich(graph(g, c))
                if i == 1 and there(g, c + 1):
                    table_rest(graph(g, c + 1), 1, less_hi, mid_done)
                if i == 2 and there(g, c):
                    copy_rich_rank(graph(g, c))
                if i == 2 and there(g, c + 1):
                    copy_rank(graph(g, c + 1), S * (2 * g + c))
                    split_bits(graph(g, c + 1), 0)
                if i == 2 and there(g, c):
                    make_weights(graph(g, c), 2 * g + c + 1, KTOT * (2 * g + c - 1), BASE)
                if i == 3 and there(g, c + 1):
                    table_rest(graph(g, c + 1), 2, less_mid, tab_done)
                if i == 3 and there(g, c - 1):
                    copy_agg_t(graph(g, c - 1))
                if i == 3 and there(g, c + 1):
                    split_bits(graph(g, c + 1), 1)
                if i == 4 and there(g, c - 1):
                    update_square(graph(g, c - 1))

        def pool_graph(g, c):
            for i in range(S):
                if there(g, c, i):
                    rsqrt(step(g, c, i)[1])
                if there(g, c, i - 1):
                    shift(step(g, c, i - 1)[1])
                if i == 0 and there(g, c - 3):
                    rstd_out(graph(g, c - 3))
                if i == 2 and there(g, c + 1):
                    make_key(graph(g, c + 1), 0, 2 * g + c + 1)
                if i == 3 and there(g, c - 2):
                    residual(graph(g, c - 2))
                if i == 4 and there(g, c - 1):
                    rstd_update(graph(g, c - 1))
                if i == 4 and there(g, c + 1):
                    make_key(graph(g, c + 1), 1, 2 * g + c + 1)

        AHEAD = ((2,), (2,), (), (1, 2), (2,))

        def dve_graph(g, c):
            for i in range(S):
                for ahead in AHEAD[i]:
                    if there(g, c, i + ahead):
                        make_onehot(*step(g, c, i + ahead))
                normed, (G, summed) = step(g, c, i - 1)[1], step(g, c, i - 3)
                agg_free = G.n - 1 if summed.h == NH else G.n - 2
                for q in range(4):
                    if there(g, c, i - 1) and q < len(normed.slots):
                        norm_slot(normed, q)
                    if there(g, c, i - 3) and q < len(summed.slots):
                        acc_slot(G, summed, q, G.n, agg_free)
                if i == 0 and there(g, c):
                    extract_first(graph(g, c), 0)
                if i == 1 and there(g, c):
                    extract_first(graph(g, c), 1)
                if i == 2 and there(g, c - 3):
                    out_norm(graph(g, c - 3))
                if i == 2 and there(g, c + 1):
                    make_places(graph(g, c + 1))
                if i == 3 and there(g, c + 1):
                    find_rich(graph(g, c + 1))
                if i == 3 and there(g, c):
                    rich_weights(graph(g, c), KTOT * (2 * g + c - 1))
                if i == 4 and there(g, c + 1):
                    number_rich(graph(g, c + 1))
                if i == 4 and there(g, c + 2):
                    make_mask(graph(g, c + 2), 2 * g + c + 1)
                if i == 4 and there(g, c + 1):
                    select_rich(graph(g, c + 1), S * (2 * g + c))
                if i == 4 and there(g, c - 2):
                    out_moments(graph(g, c - 2))

        def fast_pass(eng, one_graph):
            for c in range(-2, 4):
                one_graph(0, c)
            with eng.Fori(2, B // 2 - 1) as g:
                one_graph(g, 0)
                one_graph(g, 1)
            for c in range(5):
                one_graph(B // 2 - 1, c)


        GR = GEN_ROUNDS
        A0 = B * KTOT
        S0 = B * S
        SG = NH * GR * len(GEN_STEPS)
        AG = NH * GR * GEN_SLOTS
        GSTEP = len(GEN_STEPS)

        def gen_graph(b):
            return Graph(b, B + b + 1, 0, B // 2 + b + 1, 1, B)

        def gen_steps(b, h, r):
            for i, slots in enumerate(GEN_STEPS):
                before = sum(len(v) for v in GEN_STEPS[:i])
                yield Step(S0 + b * SG + h * (GR * GSTEP) + r * GSTEP + i,
                           A0 + b * AG + h * (GR * GEN_SLOTS) + r * GEN_SLOTS + before, i, GSTEP, i, GSTEP, h, slots)

        def gen_extraction(b, h, r):
            return B + b * (NH * GR) + h * GR + r + 1

        def gen_sp(b):
            G = gen_graph(b)
            load_adj(G, fast=False)
            load_xt(G)
            load_xt_late(G)
            load_x(G)
            store_y(G)

        def gen_pe(b):
            G = gen_graph(b)
            transpose_mask(G)
            rank_product(G, G.n - 1)
            table_product(G)
            table_less(G, 0, hi_done, less_hi)
            table_less(G, 1, mid_done, less_mid)
            for h in range(NH):
                with nc.tensor.Fori(0, GR) as r:
                    for T in gen_steps(b, h, r):
                        gather(G, T)
            transpose_agg(G, A0 + (b + 1) * AG, G.n, fast=False)
            update_product(G)

        def gen_act(b):
            G = gen_graph(b)
            copy_mask(G, B)
            copy_rank(G, S0 + b * SG)
            plus_zero(G)
            split_bits(G, 0)
            split_bits(G, 1)
            table_hi(G, S0 + b * SG)
            table_rest(G, 1, less_hi, mid_done)
            table_rest(G, 2, less_mid, tab_done)
            for h in range(NH):
                with nc.scalar.Fori(0, GR) as r:
                    make_weights(G, gen_extraction(b, h, r), A0 + b * AG + (h * GR + r) * GEN_SLOTS, EXTRACTED)
                    for T in gen_steps(b, h, r):
                        square(T)
                        gelu(T)
            copy_agg_t(G)
            update_square(G)
            update_norm(G)
            out_var(G)

        def gen_pool(b):
            G = gen_graph(b)
            make_key(G, 0, gen_extraction(b, 0, 0) - 1)
            make_key(G, 1, gen_extraction(b, 0, 0) - 1)
            for h in range(NH):
                with nc.gpsimd.Fori(0, GR) as r:
                    for T in gen_steps(b, h, r):
                        rsqrt(T)
                        shift(T)
            rstd_update(G)
            residual(G)
            rstd_out(G)

        def gen_dve(b):
            dve = nc.vector
            G = gen_graph(b)
            make_mask(G, B)
            make_places(G)
            for h in range(NH):
                dve.wait_ge(gen_slot, b * (NH * (GR + 1)) + h * (GR + 1))
                wait(dve, aggt_ps, G.n - 1)
                dve.memset(agg[:, 0, h, :], 0.0).then_inc(gen_kept, 1)
                dve.tensor_scalar(slot_no[:, :], slot_i[:, :], float(-N), None, ALU.add).then_inc(gen_slot, 1)
                with dve.Fori(0, GR) as r:
                    t = gen_extraction(b, h, r)
                    done = b * (NH * (GR + 1)) + h * (GR + 1) + r + 1
                    dve.wait_ge(gen_slot, done)
                    dve.wait_ge(gen_kept, done)
                    extract_more(G, t)
                    for T in gen_steps(b, h, r):
                        make_onehot(G, T, slot_ap=True)
                        for q in range(len(T.slots)):
                            norm_slot(T, q)
                        for q in range(len(T.slots)):
                            acc_slot(G, T, q, t)
                    dve.wait_ge(top_done, t)
                    for u in range(2):
                        last = dve.scalar_tensor_tensor(key[:, u, h, :], key[:, u, h, :], top[:, 0, h, u, GEN_SLOTS - 1:GEN_SLOTS],
                                                        key[:, u, h, :], ALU.is_lt, ALU.mult)
                    last.then_inc(gen_kept, 1)
                    dve.tensor_scalar(slot_no[:, :], slot_no[:, :], float(GEN_SLOTS), None, ALU.add).then_inc(gen_slot, 1)
            out_moments(G)
            out_norm(G)

        def general_pass(eng, one_graph, at_end=None):
            eng.wait_ge(flag_done, 1)
            more = eng.value_load(flag[0:1, 0:1], min_val=0, max_val=1)
            with eng.If(more > 0):
                with eng.Fori(0, B) as b:
                    one_graph(b)
                if at_end:
                    at_end()

        block = ctx.enter_context(nc.Block())

        @block.sync
        def _(sp):
            for dst, src in ((w1[:, :, :], W1.rearrange("(a p) o -> p a o", p=P)), (w2[:, :, :], W2.rearrange("(a p) o -> p a o", p=P)),
                             (b1r[:, :], b1.unsqueeze(0)), (b2r[:, :], b2.unsqueeze(0)),
                             (g1b[:, :], g1.partition_broadcast(P)), (be1b[:, :], be1.partition_broadcast(P)),
                             (g2b[:, :], g2.partition_broadcast(P)), (be2b[:, :], be2.partition_broadcast(P))):
                sp.dma_start(dst, src).then_inc(weights_in, 16)
            fast_pass(sp, sp_graph)
            sp.wait_ge(out_written[0], 16 * (B // 2))
            sp.wait_ge(out_written[1], 16 * (B // 2))
            general_pass(sp, gen_sp, lambda: sp.wait_ge(out_written[0], 16 * (B // 2 + B)))

        @block.gpsimd
        def _(pool):
            pool.memset(ones[:, :], 1.0)
            pool.memset(ones_row[:, :], 1.0)
            pool.memset(minus_half[:, :], -0.5)
            pool.memset(eps[:, :], LN_EPS)
            pool.memset(eps_o[:, :], LN_EPS * O)
            pool.memset(over[:, :], 0.0)
            pool.memset(ident32[:, :], 0.0)
            pool.memset(ident[:, :], 0.0)
            pool.memset(minus_ident[:, :], 0.0)
            pool.iota(order_i[:, :, :], pattern=[[0, NH], [-1, N]], base=N - 1, channel_multiplier=0)
            pool.iota(node_i[:, 0:RICH], pattern=[[1, RICH]], base=1, channel_multiplier=0)
            pool.iota(node_i[:, RICH:P], pattern=[[0, RICHEST_PARTS], [1, RICHEST]], base=1, channel_multiplier=0)
            pool.iota(rank_i[:, :, 0:RICH], pattern=[[1, RICH_SLOTS], [0, RICH]], base=BASE - N, channel_multiplier=0)
            pool.iota(rank_i[:, :, RICH:P], pattern=[[1, RICH_SLOTS], [RICH_SLOTS, RICHEST_PARTS], [0, RICHEST]], base=RICHER - N, channel_multiplier=0)
            pool.iota(slot_i[:, :], pattern=[[1, GEN_SLOTS]], base=0, channel_multiplier=0).then_inc(consts_pool, 1)
            pool.wait_ge(consts_pool, 1)
            pool.tensor_scalar(order[:, :, :], order_i[:, :, :], 65536.0, 0.0, ALU.mult, ALU.add)
            pool.affine_select(out=ident[:, :], in_=ident[:, :], compare_op=ALU.not_equal, fill=1.0, base=0, pattern=[[-1, P]], channel_multiplier=1)
            pool.affine_select(out=minus_ident[:, :], in_=minus_ident[:, :], compare_op=ALU.not_equal, fill=-1.0, base=0, pattern=[[-1, P]], channel_multiplier=1)
            pool.affine_select(out=ident32[:, :], in_=ident32[:, :], compare_op=ALU.not_equal, fill=1.0, base=0, pattern=[[-1, P]], channel_multiplier=1)
            pool.affine_select(out=upto[:, :], in_=ones[:, :], compare_op=ALU.is_ge, fill=0.0, base=0, pattern=[[1, P]], channel_multiplier=-1).then_inc(consts_pool, 1)
            pool.wait_ge(consts_pool, 2)
            pool.affine_select(out=upto_edge[:, :], in_=upto[:, :], compare_op=ALU.not_equal, fill=float(-N), base=0, pattern=[[-1, P]], channel_multiplier=1).then_inc(consts_pool, 1)
            pool.wait_ge(weights_in, 8 * 16)
            fast_pass(pool, pool_graph)
            general_pass(pool, gen_pool)

        @block.tensor
        def _(pe):
            pe.wait_ge(consts_pool, 3)
            pe.wait_ge(consts_dve, 2)
            pe.wait_ge(weights_in, 8 * 16)
            pe.wait_ge(consts_dve, 3)
            for q in range(RICH_SLOTS):
                last = pe.matmul(own_ps[:, q:q + 1], rank_no[:, q, :], ident[:, 0:1], start=True, stop=True)
            last.then_inc(own_psd, 1)
            pe.wait_ge(consts_dve, 4)
            fast_pass(pe, pe_graph)
            pe.wait_ge(over_red, 1)
            pe.transpose(end_ps[0:1, 0, 0, :], over1[:, :], ident32[:, :]).then_inc(over_t, 1)
            general_pass(pe, gen_pe)

        @block.scalar
        def _(act):
            act.wait_ge(consts_pool, 2)
            fast_pass(act, act_graph)
            general_pass(act, gen_act)

        @block.vector
        def _(dve):
            dve.wait_ge(weights_in, 8 * 16)
            dve.tensor_reduce(w1sum[:, :], w1[:, :, :], AX.X, ALU.add)
            dve.tensor_scalar(g1o[:, :], g1b[:, :], math.sqrt(O), None, ALU.mult)
            dve.tensor_scalar(g2o[:, :], g2b[:, :], math.sqrt(O), None, ALU.mult)
            dve.tensor_reduce(w2sum[:, :], w2[:, :, :], AX.X, ALU.add)
            dve.tensor_reduce(b2sum[:, :], b2r[:, :], AX.X, ALU.add)
            dve.tensor_reduce(b1sum[:, :], b1r[:, :], AX.X, ALU.add).then_inc(consts_dve, 1)
            dve.wait_ge(consts_dve, 1)
            dve.scalar_tensor_tensor(w1c[:, :, :], w1sum[:, :].unsqueeze(2).to_broadcast([P, 2, O]), -1.0 / O, w1[:, :, :], ALU.mult, ALU.add)
            dve.scalar_tensor_tensor(w2c[:, :, :], w2sum[:, :].unsqueeze(2).to_broadcast([P, 2, O]), -1.0 / O, w2[:, :, :], ALU.mult, ALU.add)
            dve.scalar_tensor_tensor(b2c[:, :], b2sum[:, :].to_broadcast([1, O]), -1.0 / O, b2r[:, :], ALU.mult, ALU.add)
            dve.memset(b1c[:, :, 0:O], 0.0)
            for h in range(NH):
                last = dve.scalar_tensor_tensor(b1c[:, h, O:2 * O], b1sum[:, :].to_broadcast([1, O]), -1.0 / O, b1r[:, :], ALU.mult, ALU.add)
            last.then_inc(consts_dve, 1)
            dve.wait_ge(consts_pool, 2)
            dve.memset(least[:, 0:1], float(BASE))
            dve.memset(least[:, 1:2], float(RICHER))
            dve.memset(limit[:, 0:NH], float(CAP))
            for h in range(NH):
                dve.memset(limit[:, NH + 2 * h:NH + 2 * h + 1], float(RICH))
                dve.memset(limit[:, NH + 2 * h + 1:NH + 2 * h + 2], float(RICHEST))
            dve.tensor_copy(node_no[:, :], node_i[:, :])
            dve.tensor_copy(rank_no[:, :, :], rank_i[:, :, :]).then_inc(consts_dve, 1)
            dve.wait_ge(consts_dve, 3)
            dve.wait_ge(own_psd, 1)
            dve.tensor_copy(own_rank[:, :], own_ps).then_inc(consts_dve, 1)
            dve.wait_ge(consts_dve, 4)
            fast_pass(dve, dve_graph)
            dve.wait_ge(over_done, B)
            dve.tensor_tensor(over_by[:, :], over[:, :], limit[:, :], ALU.subtract).then_inc(over_less, 1)
            dve.wait_ge(over_less, 1)
            dve.tensor_reduce(over1[:, :], over_by[:, :], AX.X, ALU.max).then_inc(over_red, 1)
            dve.wait_ge(over_t, 1)
            dve.tensor_reduce(over2[:, :], end_ps[0:1, 0, 0, :], AX.X, ALU.max).then_inc(over_max, 1)
            dve.wait_ge(over_max, 1)
            dve.tensor_scalar(flag[:, :], over2[:, :], 0.0, None, ALU.is_gt).then_inc(flag_done, 1)
            general_pass(dve, gen_dve)


_INS = ["x", "adj", "L0_gnn_W1", "L0_gnn_b1", "L0_gnn_g1", "L0_gnn_be1", "L0_gnn_W2", "L0_gnn_b2", "L0_gnn_g2", "L0_gnn_be2"]


def kernel(**inputs):
    import numpy as _np
    import concourse.bacc as _bacc
    from concourse import mybir as _mybir
    from concourse.bass_utils import run_bass_kernel_spmd as _run

    nc = _bacc.Bacc("TRN2", target_bir_lowering=False, num_devices=1)
    arrays, aps = {}, {}
    laid_out = {name: _np.ascontiguousarray(inputs[name]) for name in _INS}
    laid_out["xt"] = _np.ascontiguousarray(_np.transpose(laid_out["x"], (0, 2, 1)))
    for name, a in laid_out.items():
        arrays[f"in_{name}"] = a
        aps[name] = nc.dram_tensor(f"in_{name}", a.shape, _mybir.dt.from_np(a.dtype), kind="ExternalInput").ap()
    out = nc.dram_tensor("out_0", (B, N, O), _mybir.dt.float32, kind="ExternalOutput").ap()
    gnn_kernel(nc, aps["x"], aps["xt"], aps["adj"], *(aps[n] for n in _INS[2:]), out)
    r = _run(nc, [arrays], core_ids=[0])
    return r.results[0]["out_0"]
```
